# Optimizing a Trainium2 kernel written in Bass

```python
import numpy as np
import jax
import jax.numpy as jnp

def _softmax(x, axis=-1):
    return jax.nn.softmax(x, axis=axis)

def _gelu(x):
    return jax.nn.gelu(x, approximate=True)

def _silu(x):
    return jax.nn.silu(x)

def _sigmoid(x):
    return jax.nn.sigmoid(x)

def _layernorm(x, axis=-1, eps=1e-05):
    m = jnp.mean(x, axis=axis, keepdims=True)
    v = jnp.var(x, axis=axis, keepdims=True)
    return (x - m) / jnp.sqrt(v + eps)

def _scatter_add(tgt, idx, src, axis=0):
    return tgt.at[idx].add(src)

def _segment_sum(src, seg, n):
    return jax.ops.segment_sum(src, seg, n)
kernel_name = 'mk_gnn_ffn_d2_gnn_r16_216269'

def setup_inputs(seed: int=0):
    np.random.seed(seed)
    _w = jnp.asarray

    def _rec_inputs():
        import jax
        import jax.numpy as jnp
        _gk = jax.random.key(seed)
        x = -5.39e-05 + 0.9998 * jax.random.normal(jax.random.fold_in(_gk, 1), (6250, 256), jnp.float32)
        src = jax.random.randint(jax.random.fold_in(_gk, 2), (100000,), 0, 6250, jnp.int32)
        dst = jnp.minimum((6250 * jax.random.uniform(jax.random.fold_in(_gk, 3), (100000,)) ** 2.0).astype(jnp.int32), 99999)
        _o = jnp.argsort(dst, stable=True)
        src = src[_o]
        dst = dst[_o]
        edge_type_8 = jax.random.randint(jax.random.fold_in(_gk, 12), (100000,), 0, 8, jnp.int32)
        return (x, src, dst, edge_type_8)
    x, src, dst, edge_type_8 = _rec_inputs()

    def _L0_gnn_setup():
        import jax, jax.numpy as jnp
        import numpy as np
        NUM_NODES = 6250
        IN_CH = 256
        HIDDEN = 128
        OUT_CH = 256
        NUM_EDGES = 200000

        def gcn_conv(x, W, b, src, dst, num_nodes):
            h = x @ W
            loop = jnp.arange(num_nodes, dtype=src.dtype)
            s = jnp.concatenate([src, loop])
            d = jnp.concatenate([dst, loop])
            deg = jax.ops.segment_sum(jnp.ones_like(d, dtype=h.dtype), d, num_segments=num_nodes)
            dinv = jnp.where(deg > 0, jax.lax.rsqrt(deg), 0.0)
            norm = dinv[s] * dinv[d]
            msg = h[s] * norm[:, None]
            out = jax.ops.segment_sum(msg, d, num_segments=num_nodes)
            return out + b
        key = jax.random.key(seed)
        k1, k2, k3, k4 = jax.random.split(key, 4)
        edge_index = jax.random.randint(k1, (2, NUM_EDGES), 0, NUM_NODES, dtype=jnp.int64)
        node_features = jax.random.normal(k2, (NUM_NODES, IN_CH), dtype=jnp.float32)
        W1 = jax.random.normal(k3, (IN_CH, HIDDEN), dtype=jnp.float32) * (1.0 / np.sqrt(IN_CH))
        b1 = jnp.zeros((HIDDEN,), dtype=jnp.float32)
        W2 = jax.random.normal(k4, (HIDDEN, OUT_CH), dtype=jnp.float32) * (1.0 / np.sqrt(HIDDEN))
        b2 = jnp.zeros((OUT_CH,), dtype=jnp.float32)
        return {'node_features': node_features, 'W1': W1, 'b1': b1, 'W2': W2, 'b2': b2, 'edge_index': edge_index}
    _L0_gnn_all = _L0_gnn_setup()
    _L0_gnn_in = {k: v for k, v in _L0_gnn_all.items() if k in ('W1', 'b1', 'W2', 'b2')}
    del _L0_gnn_all

    def _L0_ffn_setup():
        import jax, jax.numpy as jnp
        import numpy as np
        NUM_EXPERTS = 8
        TOP_K = 2
        B, S, D = (8, 512, 256)

        def _moe(tokens, router_w, w1, b1, w2, b2):
            N = tokens.shape[0]
            E = router_w.shape[0]
            logits = tokens.astype(jnp.float32) @ router_w.astype(jnp.float32).T
            probs = jax.nn.softmax(logits, axis=-1)
            rw, re = jax.lax.top_k(probs, TOP_K)
            if TOP_K > 1:
                rw = rw / jnp.maximum(rw.sum(-1, keepdims=True), 1e-12)
            rw = rw.astype(tokens.dtype)
            combine = jnp.zeros((N, E), tokens.dtype).at[jnp.arange(N)[:, None], re].set(rw)
            out = tokens
            for e in range(E):
                h = jax.nn.gelu(tokens @ w1[e] + b1[e], approximate=False)
                y = h @ w2[e] + b2[e]
                out = out + combine[:, e:e + 1] * y
            return out
        key = jax.random.key(seed)
        ks = jax.random.split(key, 4)
        scale = 1.0 / np.sqrt(D).astype(np.float32)
        return {'input_embeddings': jax.random.normal(ks[0], (B, S, D), jnp.float32), 'router_w': jax.random.normal(ks[1], (NUM_EXPERTS, D), jnp.float32) * scale, 'w1': jax.random.normal(ks[2], (NUM_EXPERTS, D, D), jnp.float32) * scale, 'b1': jnp.zeros((NUM_EXPERTS, D), jnp.float32), 'w2': jax.random.normal(ks[3], (NUM_EXPERTS, D, D), jnp.float32) * scale, 'b2': jnp.zeros((NUM_EXPERTS, D), jnp.float32)}
    _L0_ffn_all = _L0_ffn_setup()
    _L0_ffn_in = {k: v for k, v in _L0_ffn_all.items() if k in ('router_w', 'w1', 'b1', 'w2', 'b2')}
    del _L0_ffn_all

    def _L1_gnn_setup():
        import jax, jax.numpy as jnp
        import numpy as np
        N, E, R, H, D = (1875, 18750, 8, 8, 32)
        IN_F = 256
        NEG_SLOPE = 0.2
        key = jax.random.key(seed)
        k = jax.random.split(key, 6)
        x = jax.random.normal(k[0], (N, IN_F), dtype=jnp.float32)
        W = jax.random.normal(k[1], (R, H * D, IN_F), dtype=jnp.float32) * 0.05
        attn_src = jax.random.normal(k[2], (H, D), dtype=jnp.float32) * 0.1
        attn_dst = jax.random.normal(k[3], (H, D), dtype=jnp.float32) * 0.1
        edge_index = jax.random.randint(k[4], (2, E), 0, N, dtype=jnp.int64) if jax.config.read('jax_enable_x64') else jax.random.randint(k[4], (2, E), 0, N, dtype=jnp.int32)
        edge_type = jax.random.randint(k[5], (E,), 0, R, dtype=edge_index.dtype)
        return dict(x=x, W=W, attn_src=attn_src, attn_dst=attn_dst, edge_index=edge_index, edge_type=edge_type)
    _L1_gnn_all = _L1_gnn_setup()
    _L1_gnn_in = {k: v for k, v in _L1_gnn_all.items() if k in ('W', 'attn_src', 'attn_dst')}
    del _L1_gnn_all

    def _L1_ffn_setup():
        import math
        import jax, jax.numpy as jnp
        import numpy as np
        CAPACITY_FACTOR = 1.25
        TOP_K = 2
        LN_EPS = 1e-05

        def _layer_norm(x, gamma, beta):
            mu = jnp.mean(x, axis=-1, keepdims=True)
            var = jnp.var(x, axis=-1, keepdims=True)
            return (x - mu) * jax.lax.rsqrt(var + LN_EPS) * gamma + beta
        key = jax.random.key(seed)
        ks = jax.random.split(key, 4)
        B, S, D, F, E = (8, 256, 256, 512, 8)
        x = jax.random.normal(ks[0], (B, S, D), dtype=jnp.float32)
        Wr = jax.random.normal(ks[1], (D, E), dtype=jnp.float32) / np.sqrt(D)
        br = jnp.zeros((E,), jnp.float32)
        W1 = jax.random.normal(ks[2], (E, D, F), dtype=jnp.float32) / np.sqrt(D)
        b1 = jnp.zeros((E, F), jnp.float32)
        W2 = jax.random.normal(ks[3], (E, F, D), dtype=jnp.float32) / np.sqrt(F)
        b2 = jnp.zeros((E, D), jnp.float32)
        gamma = jnp.ones((D,), jnp.float32)
        beta = jnp.zeros((D,), jnp.float32)
        return {'x': x, 'Wr': Wr, 'br': br, 'W1': W1, 'b1': b1, 'W2': W2, 'b2': b2, 'gamma': gamma, 'beta': beta}
    _L1_ffn_all = _L1_ffn_setup()
    _L1_ffn_in = {k: v for k, v in _L1_ffn_all.items() if k in ('Wr', 'br', 'W1', 'b1', 'W2', 'b2', 'gamma', 'beta')}
    del _L1_ffn_all
    return {'x': x, 'src': src, 'dst': dst, 'edge_type_8': edge_type_8, 'L0_gnn_W1': _L0_gnn_in['W1'], 'L0_gnn_b1': _L0_gnn_in['b1'], 'L0_gnn_W2': _L0_gnn_in['W2'], 'L0_gnn_b2': _L0_gnn_in['b2'], 'L0_ffn_router_w': _L0_ffn_in['router_w'], 'L0_ffn_w1': _L0_ffn_in['w1'], 'L0_ffn_b1': _L0_ffn_in['b1'], 'L0_ffn_w2': _L0_ffn_in['w2'], 'L0_ffn_b2': _L0_ffn_in['b2'], 'L1_gnn_W': _L1_gnn_in['W'], 'L1_gnn_attn_src': _L1_gnn_in['attn_src'], 'L1_gnn_attn_dst': _L1_gnn_in['attn_dst'], 'L1_ffn_Wr': _L1_ffn_in['Wr'], 'L1_ffn_br': _L1_ffn_in['br'], 'L1_ffn_W1': _L1_ffn_in['W1'], 'L1_ffn_b1': _L1_ffn_in['b1'], 'L1_ffn_W2': _L1_ffn_in['W2'], 'L1_ffn_b2': _L1_ffn_in['b2'], 'L1_ffn_gamma': _L1_ffn_in['gamma'], 'L1_ffn_beta': _L1_ffn_in['beta']}

def reference(x, src, dst, edge_type_8, L0_gnn_W1, L0_gnn_b1, L0_gnn_W2, L0_gnn_b2, L0_ffn_router_w, L0_ffn_w1, L0_ffn_b1, L0_ffn_w2, L0_ffn_b2, L1_gnn_W, L1_gnn_attn_src, L1_gnn_attn_dst, L1_ffn_Wr, L1_ffn_br, L1_ffn_W1, L1_ffn_b1, L1_ffn_W2, L1_ffn_b2, L1_ffn_gamma, L1_ffn_beta):
    import jax
    import jax.numpy as jnp

    def _L0_gnn_ref(node_features, W1, b1, W2, b2, edge_index):
        import jax, jax.numpy as jnp
        import numpy as np
        NUM_NODES = 6250
        IN_CH = 256
        HIDDEN = 128
        OUT_CH = 256
        NUM_EDGES = 200000

        def gcn_conv(x, W, b, src, dst, num_nodes):
            h = x @ W
            loop = jnp.arange(num_nodes, dtype=src.dtype)
            s = jnp.concatenate([src, loop])
            d = jnp.concatenate([dst, loop])
            deg = jax.ops.segment_sum(jnp.ones_like(d, dtype=h.dtype), d, num_segments=num_nodes)
            dinv = jnp.where(deg > 0, jax.lax.rsqrt(deg), 0.0)
            norm = dinv[s] * dinv[d]
            msg = h[s] * norm[:, None]
            out = jax.ops.segment_sum(msg, d, num_segments=num_nodes)
            return out + b
        src, dst = (edge_index[0], edge_index[1])
        x = gcn_conv(node_features, W1, b1, src, dst, NUM_NODES)
        x = jax.nn.relu(x)
        x = gcn_conv(x, W2, b2, src, dst, NUM_NODES)
        return x

    def _L0_ffn_ref(input_embeddings, router_w, w1, b1, w2, b2):
        import jax, jax.numpy as jnp
        import numpy as np
        NUM_EXPERTS = 8
        TOP_K = 2
        B, S, D = (8, 512, 256)

        def _moe(tokens, router_w, w1, b1, w2, b2):
            N = tokens.shape[0]
            E = router_w.shape[0]
            logits = tokens.astype(jnp.float32) @ router_w.astype(jnp.float32).T
            probs = jax.nn.softmax(logits, axis=-1)
            rw, re = jax.lax.top_k(probs, TOP_K)
            if TOP_K > 1:
                rw = rw / jnp.maximum(rw.sum(-1, keepdims=True), 1e-12)
            rw = rw.astype(tokens.dtype)
            combine = jnp.zeros((N, E), tokens.dtype).at[jnp.arange(N)[:, None], re].set(rw)
            out = tokens
            for e in range(E):
                h = jax.nn.gelu(tokens @ w1[e] + b1[e], approximate=False)
                y = h @ w2[e] + b2[e]
                out = out + combine[:, e:e + 1] * y
            return out
        b, s, d = input_embeddings.shape
        tokens = input_embeddings.reshape(b * s, d)
        return _moe(tokens, router_w, w1, b1, w2, b2).reshape(b, s, d)

    def _L1_gnn_ref(x, W, attn_src, attn_dst, edge_index, edge_type):
        import jax, jax.numpy as jnp
        import numpy as np
        N, E, R, H, D = (1875, 18750, 8, 8, 32)
        IN_F = 256
        NEG_SLOPE = 0.2
        n = x.shape[0]
        r = W.shape[0]
        h, d = attn_src.shape
        h_all = jnp.einsum('nf,rof->rno', x, W).reshape(r, n, h, d)
        src, dst = (edge_index[0], edge_index[1])
        h_src = h_all[edge_type, src]
        h_dst = h_all[edge_type, dst]
        scores = jnp.einsum('ehd,hd->eh', h_src, attn_src) + jnp.einsum('ehd,hd->eh', h_dst, attn_dst)
        scores = jnp.where(scores > 0, scores, NEG_SLOPE * scores)
        amax = jnp.maximum(jax.ops.segment_max(scores, dst, num_segments=n), 0.0)
        w = jnp.exp(scores - amax[dst])
        denom = jax.ops.segment_sum(w, dst, num_segments=n) + 1e-12
        w = w / denom[dst]
        msg = h_src * w[..., None]
        out = jax.ops.segment_sum(msg, dst, num_segments=n)
        return out.reshape(n, h * d)

    def _L1_ffn_ref(x, Wr, br, W1, b1, W2, b2, gamma, beta):
        import math
        import jax, jax.numpy as jnp
        import numpy as np
        CAPACITY_FACTOR = 1.25
        TOP_K = 2
        LN_EPS = 1e-05

        def _layer_norm(x, gamma, beta):
            mu = jnp.mean(x, axis=-1, keepdims=True)
            var = jnp.var(x, axis=-1, keepdims=True)
            return (x - mu) * jax.lax.rsqrt(var + LN_EPS) * gamma + beta
        B, S, D = x.shape
        E = Wr.shape[1]
        N = B * S
        K = TOP_K
        logits = jnp.mean(x, axis=1) @ Wr + br
        routing_weights = jax.nn.softmax(logits, axis=-1)
        capacity = float(math.ceil(N * CAPACITY_FACTOR / E))
        expected_loads = routing_weights.sum(axis=0) * (N / B)
        scale = jnp.where(expected_loads > capacity, capacity / expected_loads, 1.0)
        routing_weights = jax.nn.softmax(routing_weights * scale, axis=-1)
        rw_tok = jnp.broadcast_to(routing_weights[:, None, :], (B, S, E)).reshape(N, E)
        top_w, top_i = jax.lax.top_k(rw_tok, K)
        top_w = jax.nn.softmax(top_w, axis=-1)
        xf = x.reshape(N, D)
        h = jax.nn.gelu(jnp.einsum('nd,edf->enf', xf, W1) + b1[:, None, :], approximate=False)
        y = jnp.einsum('enf,efd->end', h, W2) + b2[:, None, :]
        w_dense = jnp.zeros((N, E), x.dtype).at[jnp.arange(N)[:, None], top_i].add(top_w)
        out = jnp.einsum('ne,end->nd', w_dense, y).reshape(B, S, D)
        out = _layer_norm(out + x, gamma, beta)
        return out
    edge_index = jnp.stack([src, dst])
    x = x + _L0_gnn_ref(_layernorm(x, axis=-1), L0_gnn_W1, L0_gnn_b1, L0_gnn_W2, L0_gnn_b2, edge_index)
    x = x + _L0_ffn_ref(_layernorm(x, axis=-1)[None], L0_ffn_router_w, L0_ffn_w1, L0_ffn_b1, L0_ffn_w2, L0_ffn_b2)[0]
    x = x + _L1_gnn_ref(_layernorm(x, axis=-1), L1_gnn_W, L1_gnn_attn_src, L1_gnn_attn_dst, edge_index, edge_type_8)
    x = x + _L1_ffn_ref(_layernorm(x, axis=-1)[None], L1_ffn_Wr, L1_ffn_br, L1_ffn_W1, L1_ffn_b1, L1_ffn_W2, L1_ffn_b2, L1_ffn_gamma, L1_ffn_beta)[0]
    return x

_drawn_inputs = setup_inputs


def setup_inputs(seed=0):
    import zlib

    import numpy as np

    out = dict(_drawn_inputs(seed))
    spreads = {'L0_gnn_b1': (0.0, 0.1),
     'L0_gnn_b2': (0.0, 0.1),
     'L0_ffn_b1': (0.0, 0.332),
     'L0_ffn_b2': (0.0, 0.1),
     'L1_ffn_br': (0.0, 0.8),
     'L1_ffn_b1': (0.0, 0.522),
     'L1_ffn_b2': (0.0, 0.406),
     'L1_ffn_gamma': (1.0, 0.2),
     'L1_ffn_beta': (0.0, 0.1)}
    factors = {}
    for name, (base, spread) in spreads.items():
        noise = np.random.default_rng([zlib.crc32(name.encode()), seed]).standard_normal(out[name].shape)
        drawn = base * np.exp(spread * noise) if base else spread * noise
        out[name] = jnp.asarray(drawn.astype(out[name].dtype))
    for name, factor in factors.items():
        out[name] = (out[name] * factor).astype(out[name].dtype)
    return out
```

```python
from contextlib import ExitStack

import concourse.bass as bass
from concourse import mybir

ALU = mybir.AluOpType
ACT = mybir.ActivationFunctionType
F32 = mybir.dt.float32
BF16 = mybir.dt.bfloat16
I32 = mybir.dt.int32
AX = mybir.AxisListType.X

P = 128
NODES = 6250
D = 256
KD = D // P
HID = 128
EDGES = 100000
TYPES = 8
HEADS = 8
HD = D // HEADS
EXPERTS = 8
FF = 512
NT = -(-NODES // P)
NPAD = NT * P
ET = -(-EDGES // P)
STEPS = -(-(ET + NT - 1) // 16) * 16
ETP = ET + 2
SCH = -(-(STEPS + 8) // P)
PSTEPS = SCH * P
TURNS = STEPS // 16
PAD_DST = 1 << 20
ROW = D + HEADS
GT = 7
NG = NT // GT
GH = GT * P // 2
CH = P // HEADS
CS = STEPS // CH
CW = CS * P
EPS = 1e-5
CAPACITY = float(-(-NODES * 5 // (4 * EXPERTS)))


class Signal:

    def __init__(self, ctx, nc, name):
        self.sem = ctx.enter_context(nc.semaphore(name))
        self.base = 0

    def lift(self, engine):
        engine.sem_inc(self.sem, 1)
        self.base = 1

    def wait(self, engine, n):
        engine.wait_ge(self.sem, n + self.base)
        if "SP" in str(engine.engine) and not isinstance(n, int):
            engine.nop(nofuse=True)

    def after(self, n):
        self.base += n


class Chain:

    def __init__(self, engine, counts, start=0):
        self.engine, self.counts, self.start, self.n = engine, counts, start, 0

    def did(self, instruction):
        instruction.then_inc(self.counts.sem, 1)
        self.n += 1

    def hold(self):
        self.counts.wait(self.engine, self.start + self.n)

    def step(self, instruction):
        self.did(instruction)
        self.hold()


def load_registers(engine, name, row, start, count, top):
    regs = [engine.alloc_register(f"{name}_{engine.engine.name}_{q}") for q in range(count)]
    engine.load(regs, row[0:1, bass.ds(start, count)])
    return [engine.snap(r, min_val=0, max_val=top) for r in regs]


def first_two(c, prob, iota8m, one1, one2, top1, top2, idx1, idx2, tmp, n):
    v = c.engine
    shape = [prob.shape[0], n, 8]

    def wide(x):
        return x.unsqueeze(2).to_broadcast(shape)

    def pick(src, top, idx, one):
        c.step(v.tensor_reduce(top, src, AX, ALU.max))
        c.step(v.tensor_tensor(tmp, src, wide(top), ALU.is_equal))
        c.step(v.tensor_tensor(tmp, tmp, iota8m, ALU.mult))
        c.step(v.tensor_reduce(idx, tmp, AX, ALU.min))
        c.step(v.tensor_tensor(one, iota8m, wide(idx), ALU.is_equal))

    pick(prob, top1, idx1, one1)
    c.step(v.scalar_tensor_tensor(one2, one1, -4.0, prob, ALU.mult, ALU.add))
    pick(one2, top2, idx2, one2)


def gnn_ffn_kernel(nc, x, src, dst, typ, dst_e, dst_first, g_w1, g_b1, g_w2, g_b2, m_rw, m_w1, m_b1,
                   m_w2, m_b2, a_w, a_wt, a_src, a_dst, f_wr, f_br, f_w1, f_b1, f_w2, f_b2, f_gamma,
                   f_beta, out):
    ctx = ExitStack()

    def sb(name, shape, dt=F32, where=ctx):
        return where.enter_context(nc.sbuf_tensor(name, shape, dt))

    def sig(name):
        return Signal(ctx, nc, name)

    with ctx:
        t_gcn = [nc.dram_tensor(f"t_gcn{k}", (NPAD, HID), F32, kind="Internal").ap() for k in range(2)]
        t_msg = nc.dram_tensor("t_msg", (NPAD * TYPES, ROW), F32, kind="Internal").ap()
        t_path = nc.dram_tensor("t_path", (STEPS // 8, P, 8 * D), F32, kind="Internal").ap()

        xs = sb("xs", [P, NT, D])
        idx1 = sb("idx1", [P, PSTEPS], I32)
        idx3 = sb("idx3", [P, PSTEPS], I32)
        dloc = sb("dloc", [P, PSTEPS])
        typf = sb("typf", [P, PSTEPS])
        key = sb("key", [P, PSTEPS])
        nrow = sb("nrow", [1, PSTEPS], I32)
        iota = sb("iota", [P, P])
        ident = sb("ident", [P, P])
        iota8m = sb("iota8m", [P, 8])
        ones = sb("ones", [1, P])
        dinv = sb("dinv", [P, NT])
        bn6 = sb("bn6", [P, NT, 6])
        mean = sb("mean", [P, NT])
        rstd = sb("rstd", [P, NT])
        lntmp = sb("lntmp", [P, NT])
        stage = sb("stage", [P, 16], I32)
        ps = [ctx.enter_context(nc.psum_tensor(f"ps{b}", [P, 512], F32)) for b in range(8)]

        s_in = sig("s_in")
        s_out = sig("s_out")
        s_pool = sig("s_pool")
        s_dve = sig("s_dve")
        s_act = sig("s_act")
        s_pe = sig("s_pe")
        s_row = [sig(f"s_row{j}") for j in range(16)]
        s_stage = sig("s_stage")
        s_used = sig("s_used")
        s_hot = sig("s_hot")
        s_added = sig("s_added")
        s_ld = [sig(f"s_ld{j}") for j in range(2)]
        s_a, s_b, s_c, s_d, s_e, s_f = (sig(f"s_{k}") for k in "abcdef")

        with nc.Block() as b:
            @b.vector
            def _(v):
                for s in (s_pool, s_dve, s_act, s_pe, s_stage, s_used, s_hot, s_added, s_a, s_b, s_c, s_d, s_e, s_f):
                    s.lift(v)

        with ExitStack() as ph:
            iota_i = sb("iota_i", [P, P], I32, ph)
            pcol_i = sb("pcol_i", [P, 1], I32, ph)
            step_i = sb("step_i", [P, SCH], I32, ph)
            tile_i = sb("tile_i", [1, ETP], I32, ph)
            pcol = sb("pcol", [P, 1], F32, ph)
            stepf = sb("stepf", [P, SCH], F32, ph)
            krow = sb("krow", [1, ETP], F32, ph)
            first_i = sb("first_i", [1, ETP], I32, ph)
            kall = sb("kall", [P, ETP], F32, ph)
            kcmp = sb("kcmp", [P, SCH, ETP], F32, ph)
            tf = sb("tf", [P, SCH], F32, ph)
            ti = sb("ti", [P, SCH], I32, ph)
            nf = sb("nf", [P, SCH], F32, ph)
            n128 = sb("n128", [P, SCH], F32, ph)
            raw = [[sb(f"raw{k}_{c}", [P, P], I32, ph) for c in range(SCH)] for k in range(3)]
            rowf = [[sb(f"rowf{k}_{c}", [P, P], F32, ph) for c in range(2)] for k in range(5)]
            lo_i = sb("lo_i", [P, ETP], I32, ph)
            hi_i = sb("hi_i", [P, ETP], I32, ph)
            lo_f = sb("lo_f", [P, ETP], F32, ph)
            hi_f = sb("hi_f", [P, ETP], F32, ph)
            hot_lo = [sb(f"hot_lo{k}", [P, 16, P], BF16, ph) for k in range(2)]
            hot_hi = [sb(f"hot_hi{k}", [P, 16, NT], BF16, ph) for k in range(2)]
            deg = sb("deg", [P, NT], F32, ph)
            DB = ETP // 16
            vector_steps = []

            with nc.Block() as b:
                @b.sync
                def _(sp):
                    sp.dma_start(first_i[:], dst_first).then_inc(s_in.sem, 16)
                    sp.dma_start(lo_i[:], dst_e).then_inc(s_ld[0].sem, 16)
                    s_ld[0].wait(sp, 16)
                    sp.dma_start(hi_i[:], dst_e).then_inc(s_ld[0].sem, 16)
                    xr = x.rearrange("(n p) f -> p n f", p=P)
                    for g in range(NG):
                        sp.dma_start(xs[:, g * GT:(g + 1) * GT, :], xr[:, g * GT:(g + 1) * GT, :]).then_inc(s_ld[1].sem, 16)
                    s_ld[1].wait(sp, 16 * NG)

                @b.gpsimd
                def _(g):
                    g.iota(iota_i[:], [[1, P]], base=0, channel_multiplier=0).then_inc(s_pool.sem, 1)
                    g.iota(pcol_i[:], [[0, 1]], base=0, channel_multiplier=1).then_inc(s_pool.sem, 1)
                    g.iota(step_i[:], [[P, SCH]], base=0, channel_multiplier=1).then_inc(s_pool.sem, 1)
                    g.iota(tile_i[:], [[1, ETP]], base=0, channel_multiplier=0).then_inc(s_pool.sem, 1)
                    s_c.wait(g, 1)
                    for c in range(SCH):
                        for k, a in enumerate((dst, src, typ)):
                            g.indirect_dma_start(out=raw[k][c][:], out_offset=None, in_=a,
                                                 in_offset=bass.IndirectOffsetOnAxis(ap=ti[:, c:c + 1], axis=0)
                                                 ).then_inc(s_row[c].sem, 16)

                @b.vector
                def _(v):
                    c = Chain(v, s_dve)
                    s_pool.wait(v, 4)
                    c.did(v.tensor_copy(iota[:], iota_i[:]))
                    c.did(v.tensor_copy(pcol[:], pcol_i[:]))
                    c.did(v.tensor_copy(stepf[:], step_i[:]))
                    c.did(v.tensor_copy(krow[:], tile_i[:]))
                    c.did(v.memset(ones[:], 1.0))
                    s_in.wait(v, 16)
                    c.step(v.tensor_scalar(first_i[:], first_i[:], 7, None, ALU.arith_shift_right))
                    c.did(v.tensor_scalar(ident[:], iota[:], pcol[:, 0:1], None, ALU.is_equal))
                    c.did(v.tensor_scalar(iota8m[:], iota[:, 0:8], -8.0, None, ALU.add))
                    c.step(v.tensor_scalar(first_i[:], first_i[:], float(NT - 1), None, ALU.min))
                    c.step(v.tensor_tensor(krow[:], krow[:], first_i[:], ALU.add))
                    s_pe.wait(v, 1)
                    c.did(v.tensor_copy(kall[:, 0:392], ps[0][:, 0:392]))
                    c.step(v.tensor_copy(kall[:, 392:ETP], ps[1][:, 0:ETP - 392]))
                    for k in range(SCH):
                        c.did(v.tensor_scalar(kcmp[:, k, :], kall[:], stepf[:, k:k + 1], None, ALU.is_le))
                    c.hold()
                    c.step(v.tensor_reduce(tf[:], kcmp[:, :, 1:ETP], AX, ALU.add))
                    c.did(v.tensor_tensor(nf[:], stepf[:], tf[:], ALU.subtract))
                    c.step(v.tensor_copy(ti[:], tf[:]))
                    v.tensor_scalar(n128[:], nf[:], -float(P), None, ALU.mult).then_inc(s_c.sem, 1)
                    s_c.wait(v, 1)
                    for k in range(SCH):
                        s_row[k].wait(v, 48)
                        if k >= 2:
                            s_act.wait(v, k - 1)
                        r, q = [raw[m][k][:] for m in range(3)], [rowf[m][k % 2][:] for m in range(5)]
                        c.did(v.tensor_scalar(q[0], r[0], n128[:, k:k + 1], None, ALU.add))
                        c.did(v.tensor_copy(q[1], r[0]))
                        c.did(v.tensor_copy(q[2], r[1]))
                        c.did(v.tensor_copy(q[3], r[2]))
                        c.did(v.scalar_tensor_tensor(q[4], r[1], float(TYPES), r[2], ALU.mult, ALU.add))
                        c.hold()
                        v.sem_inc(s_d.sem, 1)
                    s_ld[0].wait(v, 32)
                    c.did(v.tensor_scalar(lo_i[:], lo_i[:], P - 1, None, ALU.bitwise_and))
                    c.step(v.tensor_scalar(hi_i[:], hi_i[:], 7, None, ALU.arith_shift_right))
                    c.did(v.tensor_copy(lo_f[:], lo_i[:]))
                    c.did(v.tensor_copy(hi_f[:], hi_i[:]))
                    c.hold()
                    vector_steps.append(c.n)

                @b.tensor
                def _(t):
                    s_dve.wait(t, 10)
                    t.matmul(ps[0][:, 0:392], ones[0:1, :], krow[0:1, 0:392], start=True, stop=True)
                    t.matmul(ps[1][:, 0:ETP - 392], ones[0:1, :], krow[0:1, 392:ETP], start=True, stop=True).then_inc(s_pe.sem, 1)
                    for k in range(SCH):
                        s_d.wait(t, k + 1)
                        if k >= 1:
                            s_act.wait(t, k)
                        for m in range(4):
                            t.transpose(ps[2][:, m * P:(m + 1) * P], rowf[m][k % 2][:], ident[:])
                        t.transpose(ps[3][:, 0:P], rowf[4][k % 2][:], ident[:])
                        t.transpose(ps[3][0:1, P:2 * P], nf[:, k:k + 1], ident[:]).then_inc(s_pe.sem, 1)

                @b.scalar
                def _(a):
                    for k in range(SCH):
                        s_pe.wait(a, k + 2)
                        w = slice(k * P, (k + 1) * P)
                        for m, o in enumerate((dloc, key, idx1, typf)):
                            a.copy(o[:, w], ps[2][:, m * P:(m + 1) * P]).then_inc(s_e.sem, 1)
                        a.copy(idx3[:, w], ps[3][:, 0:P]).then_inc(s_e.sem, 1)
                        a.copy(nrow[:, w], ps[3][0:1, P:2 * P]).then_inc(s_e.sem, 1)
                        s_e.wait(a, 6 * (k + 1))
                        a.sem_inc(s_act.sem, 1)
            s_dve.after(vector_steps[0])
            s_pool.after(4)
            s_in.after(16)
            s_ld[0].after(32)
            s_ld[1].after(16 * NG)
            s_c.after(1)
            s_d.after(SCH)
            s_e.after(6 * SCH)
            s_pe.after(1 + SCH)
            s_act.after(SCH)
            for k in range(SCH):
                s_row[k].after(48)

            with nc.Block() as b:
                @b.vector
                def _(v):
                    v.memset(deg[:], 1.0).then_inc(s_dve.sem, 1)
                    with v.Fori(0, DB // GT) as i:
                        for j in range(GT):
                            first = i * GT + j
                            s_c.wait(v, i * GT + max(j - 1, 0))
                            v.tensor_tensor(hot_lo[j % 2][:], lo_f[:, bass.ds(first * 16, 16)].unsqueeze(2).to_broadcast([P, 16, P]),
                                            iota[:].unsqueeze(1).to_broadcast([P, 16, P]), ALU.is_equal).then_inc(s_a.sem, 1)
                            v.tensor_tensor(hot_hi[j % 2][:], hi_f[:, bass.ds(first * 16, 16)].unsqueeze(2).to_broadcast([P, 16, NT]),
                                            iota[:, 0:NT].unsqueeze(1).to_broadcast([P, 16, NT]), ALU.is_equal).then_inc(s_a.sem, 1)
                            s_c.wait(v, i * GT + j + 1)
                            s_dve.wait(v, i * GT + j + 1)
                            v.tensor_tensor(deg[:], deg[:], ps[j % 2][:, 0:NT], ALU.add).then_inc(s_dve.sem, 1)

                @b.tensor
                def _(t):
                    with t.Fori(0, DB // GT) as i:
                        for j in range(GT):
                            s_a.wait(t, i * 2 * GT + 2 * j + 2)
                            s_dve.wait(t, i * GT + max(j, 1))
                            for k in range(16):
                                m = t.matmul(ps[j % 2][:, 0:NT], hot_lo[j % 2][:, k, :], hot_hi[j % 2][:, k, :],
                                             start=(k == 0), stop=(k == 15))
                            m.then_inc(s_c.sem, 1)
            s_a.after(2 * DB)
            s_c.after(DB)
            s_dve.after(DB + 1)
            with nc.Block() as b:
                @b.scalar
                def _(a):
                    a.activation(deg[:], deg[:], ACT.Sqrt).then_inc(s_act.sem, 1)

                @b.vector
                def _(v):
                    s_act.wait(v, 1)
                    v.reciprocal(dinv[:], deg[:]).then_inc(s_dve.sem, 1)
            s_act.after(1)
            s_dve.after(1)

        def row_statistics():
            with nc.Block() as b:
                @b.vector
                def _(v):
                    with v.Fori(0, NG) as i:
                        for j in range(GT):
                            v.bn_stats(bn6[:, i * GT + j, :], xs[:, i * GT + j, :])

        def finish_statistics():
            with nc.Block() as b:
                @b.vector
                def _(v):
                    c = Chain(v, s_dve)
                    me, mo, ve, vo = (bn6[:, :, k] for k in (1, 4, 2, 5))
                    c.did(v.tensor_tensor(mean[:], me, mo, ALU.add))
                    c.did(v.tensor_tensor(lntmp[:], me, mo, ALU.subtract))
                    c.did(v.tensor_tensor(rstd[:], ve, vo, ALU.add))
                    c.hold()
                    c.did(v.tensor_scalar(mean[:], mean[:], 0.5, None, ALU.mult))
                    c.step(v.tensor_tensor(lntmp[:], lntmp[:], lntmp[:], ALU.mult))
                    c.step(v.scalar_tensor_tensor(rstd[:], lntmp[:], D / 4.0, rstd[:], ALU.mult, ALU.add))
                    c.step(v.tensor_scalar(rstd[:], rstd[:], 1.0 / D, EPS, ALU.mult, ALU.add))
                    s_act.wait(v, 1)
                    c.did(v.reciprocal(rstd[:], rstd[:]))
                    c.hold()
                    v.drain()

                @b.scalar
                def _(a):
                    s_dve.wait(a, 7)
                    a.activation(rstd[:], rstd[:], ACT.Sqrt).then_inc(s_act.sem, 1)
            s_dve.after(8)
            s_act.after(1)

        def gather_turns(table, slots, idx):
            def pool(g, free):
                with g.Fori(0, TURNS) as i:
                    for h in range(2):
                        s_stage.wait(g, i * 2 + h + 1)
                        free(g, i, h)
                        g.nop(nofuse=True)
                        for j in range(8 * h, 8 * h + 8):
                            g.indirect_dma_start(out=slots(j), out_offset=None, in_=table,
                                                 in_offset=bass.IndirectOffsetOnAxis(ap=stage[:, j:j + 1], axis=0)
                                                 ).then_inc(s_row[j].sem, 16)

            def act(a, free, i, h):
                free(a, i, h)
                a.copy(stage[:, 8 * h:8 * h + 8], idx[:, bass.ds(i * 16 + 8 * h, 8)]).then_inc(s_stage.sem, 1)

            return pool, act

        def after_gathers():
            s_stage.after(2 * TURNS)
            for j in range(16):
                s_row[j].after(16 * TURNS)

        def build_hot(v, buf, start):
            return v.tensor_tensor(buf, dloc[:, bass.ds(start, 8)].unsqueeze(2).to_broadcast([P, 8, P]),
                                   iota[:].unsqueeze(1).to_broadcast([P, 8, P]), ALU.is_equal)

        with ExitStack() as ph:
            acc = sb("acc", [P, NT, HID], F32, ph)
            ring = sb("ring", [P, 16, HID], F32, ph)
            hot = [sb(f"hot{k}", [P, 8, P], F32, ph) for k in range(2)]
            w1 = sb("w1", [P, KD, HID], F32, ph)
            w2 = sb("w2", [P, D], F32, ph)
            b1 = sb("b1", [P, HID], F32, ph)
            b2 = sb("b2", [1, D], F32, ph)
            xn = [sb(f"xn{k}", [P, D], F32, ph) for k in range(2)]
            xnt = [sb(f"xnt{k}", [P, D], F32, ph) for k in range(2)]

            row_statistics()
            finish_statistics()

            with nc.Block() as b:
                @b.sync
                def _(sp):
                    sp.dma_start(w1[:], g_w1.rearrange("(k p) f -> p k f", p=P)).then_inc(s_in.sem, 16)
                    sp.dma_start(w2[:], g_w2).then_inc(s_in.sem, 16)
                    sp.dma_start(b1[:], g_b1.to_broadcast([P, HID])).then_inc(s_in.sem, 16)
                    sp.dma_start(b2[:], g_b2).then_inc(s_in.sem, 16)
                    s_act.wait(sp, 2 * NT)
                    sp.dma_start(t_gcn[0].rearrange("(n p) f -> p n f", p=P), acc[:]).then_inc(s_out.sem, 16)
                    s_out.wait(sp, 16)

                @b.vector
                def _(v):
                    with v.Fori(0, NG) as i:
                        for j in range(GT):
                            n = i * GT + j
                            s_pe.wait(v, i * 2 * GT + max(2 * j - 3, 0))
                            v.tensor_scalar(xn[j % 2][:], xs[:, n, :], mean[:, bass.ds(n, 1)], rstd[:, bass.ds(n, 1)],
                                            ALU.subtract, ALU.mult).then_inc(s_dve.sem, 1)

                @b.tensor
                def _(t):
                    s_in.wait(t, 64)
                    with t.Fori(0, NG) as i:
                        for j in range(GT):
                            s_dve.wait(t, i * GT + j + 1)
                            s_act.wait(t, i * 2 * GT + max(2 * j - 3, 0))
                            for k in range(KD):
                                m = t.transpose(ps[j % 2][:, k * P:(k + 1) * P], xn[j % 2][:, k * P:(k + 1) * P], ident[:])
                            m.then_inc(s_pe.sem, 1)
                            s_act.wait(t, i * 2 * GT + 2 * j + 1)
                            for k in range(KD):
                                m = t.matmul(ps[2 + j % 2][:, 0:HID], xnt[j % 2][:, k * P:(k + 1) * P], w1[:, k, :],
                                             start=(k == 0), stop=(k == KD - 1))
                            m.then_inc(s_pe.sem, 1)

                @b.scalar
                def _(a):
                    with a.Fori(0, NG) as i:
                        for j in range(GT):
                            s_pe.wait(a, i * 2 * GT + 2 * j + 1)
                            a.copy(xnt[j % 2][:], ps[j % 2][:, 0:D]).then_inc(s_act.sem, 1)
                            s_pe.wait(a, i * 2 * GT + 2 * j + 2)
                            a.activation(acc[:, i * GT + j, :], ps[2 + j % 2][:, 0:HID], ACT.Copy,
                                         scale=dinv[:, bass.ds(i * GT + j, 1)]).then_inc(s_act.sem, 1)
            s_in.after(64)
            s_out.after(16)
            s_dve.after(NT)
            s_pe.after(2 * NT)
            s_act.after(2 * NT)

            for conv in range(2):
                with nc.Block() as b:
                    pool, stage_half = gather_turns(t_gcn[conv], lambda j: ring[:, j, :], idx1)

                    def rows_used(engine, i, h):
                        s_used.wait(engine, i * 16 + 8 * h + 8)

                    @b.gpsimd
                    def _(g):
                        pool(g, rows_used)

                    @b.scalar
                    def _(a):
                        with a.Fori(0, TURNS) as i:
                            for h in range(2):
                                stage_half(a, rows_used, i, h)

                    @b.tensor
                    def _(t):
                        t.sem_inc(s_used.sem, 16)
                        with t.Fori(0, TURNS) as i:
                            for h in range(2):
                                s_hot.wait(t, i * 2 + h + 1)
                                for j in range(8 * h, 8 * h + 8):
                                    s_row[j].wait(t, i * 16 + 16)
                                    s_added.wait(t, i * 16 + j + 1)
                                    t.matmul(ps[j % 4][:, 0:HID], hot[h][:, j % 8, :], ring[:, j, :],
                                             start=True, stop=True).then_inc(s_used.sem, 1)

                    @b.vector
                    def _(v):
                        v.sem_inc(s_added.sem, 4)
                        build_hot(v, hot[0][:], 0).then_inc(s_hot.sem, 1)
                        with v.Fori(0, TURNS) as i:
                            for h in range(2):
                                s_used.wait(v, i * 16 + 8 * h + 16)
                                build_hot(v, hot[1 - h][:], i * 16 + 8 * h + 8).then_inc(s_hot.sem, 1)
                                tiles = load_registers(v, f"c{conv}h{h}", nrow, i * 16 + 8 * h, 8, NT - 1)
                                for j in range(8 * h, 8 * h + 8):
                                    a_n = acc[:, tiles[j % 8], :]
                                    s_used.wait(v, i * 16 + j + 17)
                                    s_added.wait(v, i * 16 + j + 4)
                                    v.tensor_tensor(a_n, a_n, ps[j % 4][:, 0:HID], ALU.add).then_inc(s_added.sem, 1)
                s_used.after(STEPS + 16)
                s_added.after(STEPS + 4)
                s_hot.after(2 * TURNS + 1)
                after_gathers()
                if conv == 0:
                    with nc.Block() as b:
                        @b.vector
                        def _(v):
                            c = Chain(v, s_dve)
                            wide = [P, NT, HID]
                            dv = dinv[:].unsqueeze(2).to_broadcast(wide)
                            c.step(v.tensor_tensor(acc[:], acc[:], dv, ALU.mult))
                            c.step(v.tensor_tensor(acc[:], acc[:], b1[:].unsqueeze(1).to_broadcast(wide), ALU.add))
                            c.step(v.scalar_tensor_tensor(acc[:], acc[:], 0.0, dv, ALU.max, ALU.mult))

                        @b.sync
                        def _(sp):
                            s_dve.wait(sp, 3)
                            sp.dma_start(t_gcn[1].rearrange("(n p) f -> p n f", p=P), acc[:]).then_inc(s_out.sem, 16)
                            s_out.wait(sp, 16)
                    s_dve.after(3)
                    s_out.after(16)

            with nc.Block() as b:
                @b.vector
                def _(v):
                    with v.Fori(0, NG) as i:
                        for j in range(GT):
                            n = i * GT + j
                            s_pe.wait(v, i * 2 * GT + max(2 * j - 3, 0))
                            v.tensor_scalar(xn[j % 2][:, 0:HID], acc[:, n, :], dinv[:, bass.ds(n, 1)], None,
                                            ALU.mult).then_inc(s_a.sem, 1)
                            s_pe.wait(v, i * 2 * GT + 2 * j + 2)
                            v.tensor_tensor(xs[:, n, :], xs[:, n, :], ps[2 + j % 2][:, 0:D], ALU.add).then_inc(s_dve.sem, 1)
                            s_dve.wait(v, i * GT + j + 1)
                            v.bn_stats(bn6[:, n, :], xs[:, n, :])

                @b.tensor
                def _(t):
                    with t.Fori(0, NG) as i:
                        for j in range(GT):
                            s_a.wait(t, i * GT + j + 1)
                            s_act.wait(t, i * GT + max(j - 1, 0))
                            t.transpose(ps[j % 2][:, 0:P], xn[j % 2][:, 0:HID], ident[:]).then_inc(s_pe.sem, 1)
                            s_act.wait(t, i * GT + j + 1)
                            s_dve.wait(t, i * GT + max(j - 1, 0))
                            t.matmul(ps[2 + j % 2][:, 0:D], xnt[j % 2][:, 0:P], w2[:], start=True, stop=False)
                            t.matmul(ps[2 + j % 2][:, 0:D], ones[0:1, :], b2[0:1, :], start=False, stop=True).then_inc(s_pe.sem, 1)

                @b.scalar
                def _(a):
                    with a.Fori(0, NG) as i:
                        for j in range(GT):
                            s_pe.wait(a, i * 2 * GT + 2 * j + 1)
                            a.copy(xnt[j % 2][:, 0:P], ps[j % 2][:, 0:P]).then_inc(s_act.sem, 1)
            s_a.after(NT)
            s_dve.after(NT)
            s_pe.after(2 * NT)
            s_act.after(NT)
        finish_statistics()

        with ExitStack() as ph:
            tt = sb("tt", [P, KD, NPAD], F32, ph)
            w1 = sb("m_w1s", [P, EXPERTS, KD, D], F32, ph)
            w2 = sb("m_w2s", [P, EXPERTS, KD, D], F32, ph)
            b1 = sb("m_b1s", [P, EXPERTS, KD], F32, ph)
            b2 = sb("m_b2s", [EXPERTS, D], F32, ph)
            rw = sb("m_rws", [P, KD, EXPERTS], F32, ph)
            prob = sb("prob", [P, NT, EXPERTS], F32, ph)
            one1 = sb("one1", [P, NT, EXPERTS], F32, ph)
            one2 = sb("one2", [P, NT, EXPERTS], F32, ph)
            tmp8 = sb("tmp8", [P, NT, EXPERTS], F32, ph)
            top1, top2, i1, i2 = (sb(f"m_{k}", [P, NT], F32, ph) for k in ("top1", "top2", "i1", "i2"))
            comb, total = prob, i1
            hid = [sb(f"m_hid{k}", [P, KD, GT * P], F32, ph) for k in range(2)]
            xn = [sb(f"m_xn{k}", [P, D], F32, ph) for k in range(2)]
            xnt = [sb(f"m_xnt{k}", [P, D], F32, ph) for k in range(2)]
            cst = [sb(f"m_c{k}", [P, EXPERTS], F32, ph) for k in range(2)]
            ctt = [sb(f"m_ct{k}", [EXPERTS, P], F32, ph) for k in range(2)]

            with nc.Block() as b:
                @b.sync
                def _(sp):
                    sp.dma_start(rw[:], m_rw.rearrange("(k p) e -> p k e", p=P)).then_inc(s_in.sem, 16)
                    sp.dma_start(w1[:], m_w1.rearrange("e (k p) f -> p e k f", p=P)).then_inc(s_out.sem, 16)
                    sp.dma_start(w2[:], m_w2.rearrange("e (k p) f -> p e k f", p=P)).then_inc(s_out.sem, 16)
                    sp.dma_start(b1[:], m_b1).then_inc(s_out.sem, 16)
                    sp.dma_start(b2[:], m_b2).then_inc(s_out.sem, 16)
                    s_out.wait(sp, 64)

                @b.vector
                def _(v):
                    def normalise(i, j):
                        n = i * GT + j
                        s_a.wait(v, i * GT + max(j - 1, 0))
                        s_d.wait(v, i * GT + max(j - 1, 0))
                        v.tensor_scalar(xn[j % 2][:], xs[:, n, :], mean[:, bass.ds(n, 1)], rstd[:, bass.ds(n, 1)],
                                        ALU.subtract, ALU.mult).then_inc(s_dve.sem, 1)
                        s_dve.wait(v, i * GT + j + 1)
                        v.tensor_tensor(xs[:, n, :], xs[:, n, :], xn[j % 2][:], ALU.add).then_inc(s_d.sem, 1)

                    with v.Fori(0, NG) as i:
                        normalise(i, 0)
                        for j in range(GT):
                            if j + 1 < GT:
                                normalise(i, j + 1)
                            s_c.wait(v, i * GT + j + 1)
                            v.tensor_copy(prob[:, i * GT + j, :], ps[2 + j % 2][:, 0:EXPERTS]).then_inc(s_e.sem, 1)

                @b.scalar
                def _(a):
                    with a.Fori(0, NG) as i:
                        for j in range(GT):
                            s_a.wait(a, i * GT + j + 1)
                            s_b.wait(a, i * GT + max(j - 1, 0))
                            s_c.wait(a, i * GT + max(j - 1, 0))
                            a.copy(xnt[j % 2][:], ps[j % 2][:, 0:D]).then_inc(s_act.sem, 1)

                @b.gpsimd
                def _(g):
                    with g.Fori(0, NG) as i:
                        for j in range(GT):
                            s_act.wait(g, i * GT + j + 1)
                            g.tensor_copy(tt[:, :, bass.ds((i * GT + j) * P, P)],
                                          xnt[j % 2][:].rearrange("p (k c) -> p k c", k=KD)).then_inc(s_b.sem, 1)

                @b.tensor
                def _(t):
                    s_in.wait(t, 16)

                    def turn_rows(i, j):
                        s_dve.wait(t, i * GT + j + 1)
                        s_act.wait(t, i * GT + max(j - 1, 0))
                        for k in range(KD):
                            m = t.transpose(ps[j % 2][:, k * P:(k + 1) * P], xn[j % 2][:, k * P:(k + 1) * P], ident[:])
                        m.then_inc(s_a.sem, 1)

                    with t.Fori(0, NG) as i:
                        turn_rows(i, 0)
                        for j in range(GT):
                            if j + 1 < GT:
                                turn_rows(i, j + 1)
                            s_act.wait(t, i * GT + j + 1)
                            s_e.wait(t, i * GT + max(j - 1, 0))
                            for k in range(KD):
                                m = t.matmul(ps[2 + j % 2][:, 0:EXPERTS], xnt[j % 2][:, k * P:(k + 1) * P], rw[:, k, :],
                                             start=(k == 0), stop=(k == KD - 1))
                            m.then_inc(s_c.sem, 1)
            s_in.after(16)
            s_out.after(64)
            for s in (s_a, s_b, s_c, s_d, s_e, s_dve, s_act):
                s.after(NT)

            with nc.Block() as b:
                vector_steps = []
                wide = [P, NT, EXPERTS]

                @b.vector
                def _(v):
                    c = Chain(v, s_dve)
                    c.step(v.tensor_reduce(top1[:], prob[:], AX, ALU.max))
                    c.step(v.tensor_tensor(prob[:], prob[:], top1[:].unsqueeze(2).to_broadcast(wide), ALU.subtract))
                    s_act.wait(v, 1)
                    c.step(v.tensor_reduce(total[:], prob[:], AX, ALU.add))
                    c.step(v.reciprocal(total[:], total[:]))
                    c.step(v.tensor_tensor(prob[:], prob[:], total[:].unsqueeze(2).to_broadcast(wide), ALU.mult))
                    first_two(c, prob[:], iota8m[:].unsqueeze(1).to_broadcast(wide), one1[:], one2[:], top1[:], top2[:],
                              i1[:], i2[:], tmp8[:], NT)
                    c.step(v.tensor_tensor(total[:], top1[:], top2[:], ALU.add))
                    c.step(v.tensor_scalar(total[:], total[:], 1e-12, None, ALU.max))
                    c.step(v.reciprocal(total[:], total[:]))
                    c.did(v.tensor_tensor(one1[:], one1[:], top1[:].unsqueeze(2).to_broadcast(wide), ALU.mult))
                    c.did(v.tensor_tensor(one2[:], one2[:], top2[:].unsqueeze(2).to_broadcast(wide), ALU.mult))
                    c.hold()
                    c.step(v.tensor_tensor(one1[:], one1[:], one2[:], ALU.add))
                    c.step(v.tensor_tensor(comb[:], one1[:], total[:].unsqueeze(2).to_broadcast(wide), ALU.mult))
                    vector_steps.append(c.n)

                @b.scalar
                def _(a):
                    s_dve.wait(a, 2)
                    a.activation(prob[:], prob[:], ACT.Exp).then_inc(s_act.sem, 1)
            s_dve.after(vector_steps[0])
            s_act.after(1)

            UE = 2 * KD
            with nc.Block() as b:
                @b.tensor
                def _(t):
                    def up(i, e):
                        for u in range(UE):
                            f, q = divmod(u, 2)
                            s_act.wait(t, i * (UE * EXPERTS) + max(UE * (e - 1) + u + 1, 0))
                            for k in range(KD):
                                m = t.matmul(ps[u][:, 0:GH], w1[:, e, k, f * P:(f + 1) * P],
                                             tt[:, k, bass.ds(i * (GT * P) + q * GH, GH)], start=(k == 0), stop=(k == KD - 1))
                            m.then_inc(s_a.sem, 1)

                    def down(i, e):
                        for j in range(GT):
                            item = GT * e + j
                            if j == 0:
                                s_act.wait(t, i * (UE * EXPERTS) + UE * (e + 1))
                            s_dve.wait(t, i * (GT * EXPERTS) + max(item - 3, 0))
                            for k in range(KD):
                                m = t.matmul(ps[4 + item % 4][:, 0:D], hid[e % 2][:, k, j * P:(j + 1) * P], w2[:, e, k, :],
                                             start=(k == 0), stop=(k == KD - 1))
                            m.then_inc(s_b.sem, 1)

                    with t.Fori(0, NG) as i:
                        for j in range(GT):
                            s_c.wait(t, i * GT + j + 1)
                            s_e.wait(t, i * GT + max(j - 1, 0))
                            t.transpose(ps[j % 2][0:EXPERTS, 0:P], cst[j % 2][:], ident[:]).then_inc(s_pe.sem, 1)
                            s_d.wait(t, i * GT + j + 1)
                            t.matmul(ps[2 + j % 2][:, 0:D], ctt[j % 2][:], b2[:], start=True, stop=True).then_inc(s_f.sem, 1)
                        s_e.wait(t, i * GT + GT)
                        up(i, 0)
                        for e in range(EXPERTS):
                            if e + 1 < EXPERTS:
                                up(i, e + 1)
                            down(i, e)

                @b.scalar
                def _(a):
                    with a.Fori(0, NG) as i:
                        for j in range(GT):
                            s_pe.wait(a, i * GT + max(j - 1, 0))
                            a.copy(cst[j % 2][:], comb[:, i * GT + j, :]).then_inc(s_c.sem, 1)
                            s_pe.wait(a, i * GT + j + 1)
                            a.copy(ctt[j % 2][:], ps[j % 2][0:EXPERTS, 0:P]).then_inc(s_d.sem, 1)
                        for e in range(EXPERTS):
                            for u in range(UE):
                                f, q = divmod(u, 2)
                                s_a.wait(a, i * (UE * EXPERTS) + UE * e + u + 1)
                                if e >= 2:
                                    s_b.wait(a, i * (GT * EXPERTS) + GT * (e - 1))
                                a.activation(hid[e % 2][:, f, q * GH:(q + 1) * GH], ps[u][:, 0:GH], ACT.Gelu,
                                             bias=b1[:, e, f:f + 1]).then_inc(s_act.sem, 1)

                @b.vector
                def _(v):
                    with v.Fori(0, NG) as i:
                        for j in range(GT):
                            n = i * GT + j
                            s_f.wait(v, i * GT + j + 1)
                            v.tensor_tensor(xs[:, n, :], xs[:, n, :], ps[2 + j % 2][:, 0:D], ALU.add).then_inc(s_e.sem, 1)
                        s_e.wait(v, i * GT + GT)
                        for e in range(EXPERTS):
                            for j in range(GT):
                                n, item = i * GT + j, GT * e + j
                                s_b.wait(v, i * (GT * EXPERTS) + item + 1)
                                if e:
                                    s_dve.wait(v, i * (GT * EXPERTS) + item - GT + 1)
                                v.scalar_tensor_tensor(xs[:, n, :], ps[4 + item % 4][:, 0:D], comb[:, n, e:e + 1],
                                                       xs[:, n, :], ALU.mult, ALU.add).then_inc(s_dve.sem, 1)
                        s_dve.wait(v, i * (GT * EXPERTS) + GT * EXPERTS)
                        for j in range(GT):
                            n = i * GT + j
                            v.bn_stats(bn6[:, n, :], xs[:, n, :])
            for s in (s_c, s_d, s_e, s_f, s_pe):
                s.after(NT)
            s_a.after(NG * UE * EXPERTS)
            s_act.after(NG * UE * EXPERTS)
            s_b.after(NT * EXPERTS)
            s_dve.after(NT * EXPERTS)
        finish_statistics()

        with ExitStack() as l1:
            weight = sb("weight", [P, STEPS, HEADS], F32, l1)
            flat = STEPS * HEADS
            sc = weight[:].rearrange("p s h -> p (s h)")

            with ExitStack() as l1a:
                sdst = sb("sdst", [P, NT, TYPES * HEADS], F32, l1a)
                scd = sb("scd", [P, STEPS, HEADS], F32, l1a)

                with ExitStack() as ph:
                    wt = sb("a_wts", [P, KD, TYPES * D], F32, ph)
                    wn = sb("a_wn", [P, TYPES, KD, D], F32, ph)
                    at = sb("a_at", [P, KD, 2 * HEADS], F32, ph)
                    wa = sb("a_wa", [P, KD, 2 * TYPES * HEADS], F32, ph)
                    xn = [sb(f"a_xn{k}", [P, D], F32, ph) for k in range(2)]
                    xnt = [sb(f"a_xnt{k}", [P, D], F32, ph) for k in range(2)]
                    rows = [sb(f"a_rows{k}", [P, TYPES, ROW], F32, ph) for k in range(2)]
                    with nc.Block() as b:
                        @b.vector
                        def _(v):
                            v.memset(at[:], 0.0).then_inc(s_dve.sem, 1)

                        @b.sync
                        def _(sp):
                            sp.dma_start(wt[:], a_wt.rearrange("(k p) r o -> p k (r o)", p=P)).then_inc(s_in.sem, 16)
                            sp.dma_start(wn[:], a_w.rearrange("r (k p) f -> p r k f", p=P)).then_inc(s_in.sem, 16)
                            s_dve.wait(sp, 1)
                            for h in range(HEADS):
                                k, r = divmod(h * HD, P)
                                for m, a in enumerate((a_src, a_dst)):
                                    sp.dma_start(at[r:r + HD, k, m * HEADS + h:m * HEADS + h + 1], a[h]).then_inc(s_in.sem, 16)
                            s_in.wait(sp, 16 * (2 + 2 * HEADS))
                    s_in.after(16 * (2 + 2 * HEADS))
                    s_dve.after(1)

                    with nc.Block() as b:
                        @b.tensor
                        def _(t):
                            for k in range(KD):
                                for r in range(TYPES):
                                    for o in range(KD):
                                        m = t.matmul(ps[k][:, r * 2 * HEADS:(r + 1) * 2 * HEADS], wn[:, r, o, k * P:(k + 1) * P],
                                                     at[:, o, :], start=(o == 0), stop=(o == KD - 1))
                                m.then_inc(s_pe.sem, 1)

                        @b.vector
                        def _(v):
                            for k in range(KD):
                                s_pe.wait(v, k + 1)
                                v.tensor_copy(wa[:, k, :].rearrange("p (m r h) -> p r m h", m=2, r=TYPES),
                                              ps[k][:, 0:2 * HEADS * TYPES].rearrange("p (r m h) -> p r m h", m=2, r=TYPES))
                    s_pe.after(KD)

                    QB = TYPES * D // 512

                    def rows_stored(engine, i, j):
                        s_ld[j % 2].wait(engine, i * (16 * (4 - j % 2)) + 16 * (j // 2))

                    with nc.Block() as b:
                        @b.vector
                        def _(v):
                            def normalise(i, j):
                                n = i * GT + j
                                s_a.wait(v, i * GT + max(j - 1, 0))
                                v.tensor_scalar(xn[j % 2][:], xs[:, n, :], mean[:, bass.ds(n, 1)], rstd[:, bass.ds(n, 1)],
                                                ALU.subtract, ALU.mult).then_inc(s_dve.sem, 1)

                            with v.Fori(0, NG) as i:
                                normalise(i, 0)
                                for j in range(GT):
                                    if j + 1 < GT:
                                        normalise(i, j + 1)
                                    for q in range(2):
                                        s_c.wait(v, i * (GT * QB) + QB * j + 2 * q + 2)
                                        if q == 0:
                                            rows_stored(v, i, j)
                                        v.tensor_copy(rows[j % 2][:, 4 * q + 2:4 * q + 4, 0:D],
                                                      ps[2 + 2 * q + 1][:].rearrange("p (r o) -> p r o", r=2)).then_inc(s_b.sem, 1)
                                    s_d.wait(v, i * GT + j + 1)
                                    v.tensor_copy(rows[j % 2][:, :, D:ROW],
                                                  ps[6 + j % 2][:, 0:64].rearrange("p (r h) -> p r h", r=TYPES)).then_inc(s_b.sem, 1)
                                    v.tensor_copy(sdst[:, i * GT + j, :], ps[6 + j % 2][:, 64:128]).then_inc(s_b.sem, 1)

                        @b.scalar
                        def _(a):
                            with a.Fori(0, NG) as i:
                                for j in range(GT):
                                    s_a.wait(a, i * GT + j + 1)
                                    s_d.wait(a, i * GT + max(j - 1, 0))
                                    a.copy(xnt[j % 2][:], ps[j % 2][:, 0:D]).then_inc(s_act.sem, 1)
                                    for q in range(2):
                                        s_c.wait(a, i * (GT * QB) + QB * j + 2 * q + 1)
                                        if q == 0:
                                            rows_stored(a, i, j)
                                        a.copy(rows[j % 2][:, 4 * q:4 * q + 2, 0:D],
                                               ps[2 + 2 * q][:].rearrange("p (r o) -> p r o", r=2)).then_inc(s_f.sem, 1)

                        @b.tensor
                        def _(t):
                            def turn_rows(i, j):
                                s_dve.wait(t, i * GT + j + 1)
                                s_act.wait(t, i * GT + max(j - 1, 0))
                                for k in range(KD):
                                    m = t.transpose(ps[j % 2][:, k * P:(k + 1) * P], xn[j % 2][:, k * P:(k + 1) * P], ident[:])
                                m.then_inc(s_a.sem, 1)

                            with t.Fori(0, NG) as i:
                                turn_rows(i, 0)
                                for j in range(GT):
                                    s_act.wait(t, i * GT + j + 1)
                                    for q in range(QB):
                                        if q % 2 == 0:
                                            s_f.wait(t, i * (2 * GT) + max(2 * j + q // 2 - 1, 0))
                                        else:
                                            s_b.wait(t, i * (4 * GT) + max(4 * j + q // 2 - 3, 0))
                                        for k in range(KD):
                                            m = t.matmul(ps[2 + q][:], xnt[j % 2][:, k * P:(k + 1) * P],
                                                         wt[:, k, q * 512:(q + 1) * 512], start=(k == 0), stop=(k == KD - 1))
                                        m.then_inc(s_c.sem, 1)
                                        if q == 1 and j + 1 < GT:
                                            turn_rows(i, j + 1)
                                    s_b.wait(t, i * (4 * GT) + max(4 * j - 4, 0))
                                    for k in range(KD):
                                        m = t.matmul(ps[6 + j % 2][:, 0:P], xnt[j % 2][:, k * P:(k + 1) * P], wa[:, k, :],
                                                     start=(k == 0), stop=(k == KD - 1))
                                    m.then_inc(s_d.sem, 1)

                        @b.sync
                        def _(sp):
                            view = t_msg.rearrange("(n p r) w -> n p r w", p=P, r=TYPES)
                            with sp.Fori(0, NG) as i:
                                for j in range(GT):
                                    s_b.wait(sp, i * (4 * GT) + 4 * j + 4)
                                    s_f.wait(sp, i * (2 * GT) + 2 * j + 2)
                                    sp.dma_start(view[i * GT + j], rows[j % 2][:]).then_inc(s_ld[j % 2].sem, 16)
                            s_ld[0].wait(sp, 16 * 4 * NG)
                            s_ld[1].wait(sp, 16 * 3 * NG)
                    for s in (s_dve, s_a, s_act, s_d):
                        s.after(NT)
                    s_b.after(4 * NT)
                    s_f.after(2 * NT)
                    s_c.after(QB * NT)
                    s_ld[0].after(16 * 4 * NG)
                    s_ld[1].after(16 * 3 * NG)

                with ExitStack() as ph:
                    ring = sb("a_ring", [P, 16, ROW], F32, ph)
                    hot = sb("a_hot", [P, 8, P], F32, ph)
                    hott = sb("a_hott", [P, 8, P], F32, ph)
                    tmask = sb("a_tmask", [P, 8, TYPES], F32, ph)
                    prod = sb("a_prod", [P, 8, TYPES, HEADS], F32, ph)
                    iota8 = sb("a_iota8", [P, TYPES], F32, ph)
                    with nc.Block() as b:
                        @b.vector
                        def _(v):
                            v.tensor_scalar(iota8[:], iota8m[:], 8.0, None, ALU.add)

                    with nc.Block() as b:
                        pool, stage_half = gather_turns(t_msg, lambda j: ring[:, j, :], idx3)

                        def rows_used(engine, i, h):
                            s_used.wait(engine, i * 2 + h + 1)

                        @b.gpsimd
                        def _(g):
                            pool(g, rows_used)

                        @b.sync
                        def _(sp):
                            sp.sem_inc(s_used.sem, 2)
                            with sp.Fori(0, TURNS) as i:
                                for h in range(2):
                                    for j in range(8 * h, 8 * h + 8):
                                        s_row[j].wait(sp, i * 16 + 16)
                                    sp.dma_start(t_path[i * 2 + h].rearrange("p (s f) -> p s f", s=8),
                                                 ring[:, 8 * h:8 * h + 8, 0:D]).then_inc(s_ld[h].sem, 16)
                                    s_ld[h].wait(sp, i * 16 + 16)
                                    s_c.wait(sp, i * 2 + h + 1)
                                    sp.sem_inc(s_used.sem, 1)

                        @b.scalar
                        def _(a):
                            def copy_terms(i, h):
                                for j in range(8 * h, 8 * h + 8):
                                    s_row[j].wait(a, i * 16 + 16)
                                a.copy(weight[:, bass.ds(i * 16 + 8 * h, 8), :],
                                       ring[:, 8 * h:8 * h + 8, D:ROW]).then_inc(s_c.sem, 1)

                            with a.Fori(0, TURNS) as i:
                                for h in range(2):
                                    stage_half(a, rows_used, i, h)
                                for h in range(2):
                                    s_a.wait(a, i * 2 + h + 1)
                                    s_b.wait(a, i * 2 + h)
                                    for q in range(2):
                                        a.copy(hott[:, 4 * q:4 * q + 4, :],
                                               ps[q][:].rearrange("p (s c) -> p s c", s=4)).then_inc(s_act.sem, 1)
                                    copy_terms(i, h)

                        @b.tensor
                        def _(t):
                            with t.Fori(0, TURNS) as i:
                                for h in range(2):
                                    s_hot.wait(t, i * 2 + h + 1)
                                    s_act.wait(t, i * 4 + 2 * h)
                                    for j in range(8):
                                        m = t.transpose(ps[j // 4][:, (j % 4) * P:(j % 4 + 1) * P], hot[:, j, :], ident[:])
                                    m.then_inc(s_a.sem, 1)
                                    tiles = load_registers(t, f"s{h}", nrow, i * 16 + 8 * h, 8, NT - 1)
                                    s_act.wait(t, i * 4 + 2 * h + 2)
                                    s_d.wait(t, i * 2 + max(h - 1, 0))
                                    for j in range(8):
                                        m = t.matmul(ps[2 + h][:, j * 64:(j + 1) * 64], hott[:, j, :], sdst[:, tiles[j], :],
                                                     start=True, stop=True)
                                    m.then_inc(s_b.sem, 1)

                        @b.vector
                        def _(v):
                            wide = [P, 8, TYPES, HEADS]
                            with v.Fori(0, TURNS) as i:
                                for h in range(2):
                                    s_a.wait(v, i * 2 + h)
                                    build_hot(v, hot[:], i * 16 + 8 * h).then_inc(s_hot.sem, 1)
                                    s_d.wait(v, i * 2 + h)
                                    v.tensor_tensor(tmask[:], typf[:, bass.ds(i * 16 + 8 * h, 8)].unsqueeze(2).to_broadcast([P, 8, TYPES]),
                                                    iota8[:].unsqueeze(1).to_broadcast([P, 8, TYPES]), ALU.is_equal).then_inc(s_e.sem, 1)
                                    s_e.wait(v, i * 2 + h + 1)
                                    s_b.wait(v, i * 2 + h + 1)
                                    s_f.wait(v, i * 2 + h)
                                    v.tensor_tensor(prod[:], ps[2 + h][:].rearrange("p (s r h) -> p s r h", s=8, r=TYPES),
                                                    tmask[:].unsqueeze(3).to_broadcast(wide), ALU.mult).then_inc(s_d.sem, 1)
                                    s_d.wait(v, i * 2 + h + 1)
                                    v.tensor_reduce(scd[:, bass.ds(i * 16 + 8 * h, 8), :], prod[:].rearrange("p s r h -> p s h r"),
                                                    AX, ALU.add).then_inc(s_f.sem, 1)
                    s_used.after(2 * TURNS + 2)
                    after_gathers()
                    s_ld[0].after(16 * TURNS)
                    s_ld[1].after(16 * TURNS)
                    for s in (s_a, s_b, s_c, s_d, s_e, s_f, s_hot):
                        s.after(2 * TURNS)
                    s_act.after(4 * TURNS)

                with ExitStack() as ph:
                    score = sb("score", [P, CW], F32, ph)
                    keyt = sb("keyt", [P, CW], F32, ph)
                    stg = sb("stg", [P, 4, P], F32, ph)
                    stk = sb("stk", [P, 4, P], F32, ph)
                    valid = sb("valid", [P, STEPS], F32, ph)
                    carry = [sb(f"carry{k}", [1, P], F32, ph) for k in range(13)]
                    cols = sb("cols", [P, 2], F32, ph)
                    Q = CS // 4

                    def by_chunk(a, i, n=HEADS):
                        return a.rearrange("p (c j) h -> p j c h", c=CH)[:, bass.ds(i * 4, 4), :, :]

                    with nc.Block() as b:
                        @b.vector
                        def _(v):
                            c = Chain(v, s_dve)
                            c.step(v.tensor_scalar(valid[:], dloc[:, 0:STEPS], 0.0, None, ALU.is_ge))
                            c.step(v.scalar_tensor_tensor(valid[:], dloc[:, 0:STEPS], float(P - 1), valid[:], ALU.is_le, ALU.mult))
                            c.step(v.tensor_tensor(weight[:], weight[:], valid[:].unsqueeze(2).to_broadcast([P, STEPS, HEADS]), ALU.mult))
                            c.step(v.tensor_tensor(weight[:], weight[:], scd[:], ALU.add))
                            c.step(v.scalar_tensor_tensor(scd[:], weight[:], 0.2, weight[:], ALU.mult, ALU.max))
                    s_dve.after(5)
                    with nc.Block() as b:
                        @b.vector
                        def _(v):
                            with v.Fori(0, Q) as i:
                                s_a.wait(v, i)
                                v.tensor_copy(stg[:].rearrange("p j (c h) -> p j c h", c=CH), by_chunk(scd[:], i)).then_inc(s_dve.sem, 1)
                                v.tensor_copy(stk[:].rearrange("p j (c h) -> p j c h", c=CH),
                                              by_chunk(key[:, 0:STEPS].unsqueeze(2).to_broadcast([P, STEPS, HEADS]), i)).then_inc(s_dve.sem, 1)

                        @b.tensor
                        def _(t):
                            with t.Fori(0, Q) as i:
                                s_dve.wait(t, i * 2 + 2)
                                s_act.wait(t, i * 2)
                                for k, s in enumerate((stg, stk)):
                                    for j in range(4):
                                        m = t.transpose(ps[k][:, j * P:(j + 1) * P], s[:, j, :], ident[:])
                                m.then_inc(s_a.sem, 1)

                        @b.scalar
                        def _(a):
                            with a.Fori(0, Q) as i:
                                s_a.wait(a, i + 1)
                                a.copy(score[:, bass.ds(i * 512, 512)], ps[0][:]).then_inc(s_act.sem, 1)
                                a.copy(keyt[:, bass.ds(i * 512, 512)], ps[1][:]).then_inc(s_act.sem, 1)
                    s_a.after(Q)
                    s_dve.after(2 * Q)
                    s_act.after(2 * Q)

                    same, seg = sc, scd[:].rearrange("p s h -> p (s h)")
                    kf, kl, lf, fb, one, link, linkr, fwd, bwd, left, right, lcol, rcol = (c[:] for c in carry)
                    hc = "a (h c) -> a h c"

                    def r3(a):
                        return a.rearrange(hc, h=HEADS)

                    vector_steps = []
                    with nc.Block() as b:
                        @b.vector
                        def _(v):
                            c = Chain(v, s_dve)
                            c.did(v.memset(same[:, 0:1], 0.0))
                            c.step(v.tensor_tensor(same[:, 1:CW], keyt[:, 1:CW], keyt[:, 0:CW - 1], ALU.is_equal))
                            c.step(v.tensor_tensor_scan(seg, same, score[:], 0.0, ALU.mult, ALU.max))
                            c.step(v.tensor_copy(cols[:, 0:1], seg[:, CW - 1:CW]))
                            c.step(v.tensor_tensor_scan(seg[:, 0:CW - 1][:, ::-1], same[:, 1:CW][:, ::-1], seg[:, 0:CW - 1][:, ::-1],
                                                        seg[:, CW - 1:CW], ALU.mult, ALU.max))
                            s_pe.wait(v, 1)
                            for k, r in enumerate((kf, kl, lf, fb)):
                                c.did(v.tensor_copy(r3(r), ps[0][0:1, k * P:(k + 1) * P].rearrange("a (c h) -> a h c", h=HEADS)))
                            for r in (link, linkr, left, right):
                                c.did(v.memset(r, 0.0))
                            c.hold()
                            c.step(v.tensor_tensor(one, kf, kl, ALU.is_equal))
                            c.did(v.tensor_tensor(r3(link)[:, :, 1:CH], r3(kf)[:, :, 1:CH], r3(kl)[:, :, 0:CH - 1], ALU.is_equal))
                            c.did(v.tensor_tensor(r3(linkr)[:, :, 0:CH - 1], r3(kf)[:, :, 1:CH], r3(kl)[:, :, 0:CH - 1], ALU.is_equal))
                            c.hold()
                            c.did(v.tensor_tensor(lcol, one, link, ALU.mult))
                            c.did(v.tensor_tensor(rcol, one, linkr, ALU.mult))
                            c.hold()
                            c.did(v.tensor_tensor_scan(fwd, lcol, lf, 0.0, ALU.mult, ALU.max))
                            c.did(v.tensor_tensor_scan(bwd[:, ::-1], rcol[:, ::-1], fb[:, ::-1], 0.0, ALU.mult, ALU.max))
                            c.hold()
                            c.did(v.tensor_tensor(r3(left)[:, :, 1:CH], r3(link)[:, :, 1:CH], r3(fwd)[:, :, 0:CH - 1], ALU.mult))
                            c.did(v.tensor_tensor(r3(right)[:, :, 0:CH - 1], r3(linkr)[:, :, 0:CH - 1], r3(bwd)[:, :, 1:CH], ALU.mult))
                            c.hold()
                            c.did(v.tensor_copy(lcol.rearrange("a (c h) -> a c h", h=HEADS), left.rearrange("a (h c) -> a c h", h=HEADS)))
                            c.did(v.tensor_copy(rcol.rearrange("a (c h) -> a c h", h=HEADS), right.rearrange("a (h c) -> a c h", h=HEADS)))
                            c.hold()
                            v.sem_inc(s_a.sem, 1)
                            s_pe.wait(v, 2)
                            c.step(v.tensor_copy(cols[:], ps[1][:, 0:2]))
                            for k, at_ in ((0, slice(0, 1)), (1, slice(CW - 1, CW))):
                                c.step(v.tensor_scalar(same, keyt[:], keyt[:, at_], cols[:, k:k + 1], ALU.is_equal, ALU.mult))
                                c.step(v.tensor_tensor(seg, seg, same, ALU.max))
                            c.step(v.tensor_tensor(score[:], score[:], seg, ALU.subtract))
                            vector_steps.append(c.n)

                        @b.tensor
                        def _(t):
                            s_dve.wait(t, 5)
                            for k, a in enumerate((keyt[:, 0:1], keyt[:, CW - 1:CW], cols[:, 0:1], seg[:, 0:1])):
                                m = t.transpose(ps[0][0:1, k * P:(k + 1) * P], a, ident[:])
                            m.then_inc(s_pe.sem, 1)
                            s_a.wait(t, 1)
                            t.transpose(ps[1][:, 0:1], lcol, ident[0:1, 0:1])
                            t.transpose(ps[1][:, 1:2], rcol, ident[0:1, 0:1]).then_inc(s_pe.sem, 1)
                    s_dve.after(vector_steps[0])
                    s_a.after(1)
                    s_pe.after(2)

                    with nc.Block() as b:
                        @b.scalar
                        def _(a):
                            with a.Fori(0, Q) as i:
                                s_a.wait(a, i)
                                a.activation(stg[:].rearrange("p j c -> p (j c)"), score[:, bass.ds(i * 512, 512)],
                                             ACT.Exp).then_inc(s_act.sem, 1)

                        @b.tensor
                        def _(t):
                            with t.Fori(0, Q) as i:
                                s_act.wait(t, i + 1)
                                s_dve.wait(t, i)
                                for j in range(4):
                                    m = t.transpose(ps[0][:, j * P:(j + 1) * P], stg[:, j, :], ident[:])
                                m.then_inc(s_a.sem, 1)

                        @b.vector
                        def _(v):
                            with v.Fori(0, Q) as i:
                                s_a.wait(v, i + 1)
                                v.tensor_copy(by_chunk(weight[:], i),
                                              ps[0][:].rearrange("p (j c h) -> p j c h", j=4, c=CH)).then_inc(s_dve.sem, 1)
                    s_a.after(Q)
                    s_act.after(Q)
                    s_dve.after(Q)

            with ExitStack() as ph:
                acc = sb("a_acc", [P, NT, ROW], F32, ph)
                raws = [sb(f"a_raw{k}", [P, 8, D], F32, ph) for k in range(2)]
                msgs = [sb(f"a_msg{k}", [P, 8, ROW], F32, ph) for k in range(2)]
                hot = [sb(f"a_hot2{k}", [P, 8, P], F32, ph) for k in range(2)]
                with nc.Block() as b:
                    @b.vector
                    def _(v):
                        v.memset(acc[:], 0.0)

                with nc.Block() as b:
                    @b.sync
                    def _(sp):
                        with sp.Fori(0, TURNS) as i:
                            for h in range(2):
                                s_a.wait(sp, i * 2 + max(h - 1, 0))
                                sp.dma_start(raws[h][:].rearrange("p s f -> p (s f)"), t_path[i * 2 + h]).then_inc(s_ld[h].sem, 16)

                    @b.scalar
                    def _(a):
                        with a.Fori(0, TURNS) as i:
                            for h in range(2):
                                s_used.wait(a, i * 16 + 8 * h + 8)
                                a.copy(msgs[h][:, :, D:ROW], weight[:, bass.ds(i * 16 + 8 * h, 8), :]).then_inc(s_act.sem, 1)

                    @b.tensor
                    def _(t):
                        t.sem_inc(s_used.sem, 16)
                        with t.Fori(0, TURNS) as i:
                            for h in range(2):
                                s_hot.wait(t, i * 2 + h + 1)
                                s_a.wait(t, i * 2 + h + 1)
                                s_act.wait(t, i * 2 + h + 1)
                                for j in range(8 * h, 8 * h + 8):
                                    s_added.wait(t, i * 16 + j + 1)
                                    t.matmul(ps[j % 4][:, 0:ROW], hot[h][:, j % 8, :], msgs[h][:, j % 8, :],
                                             start=True, stop=True).then_inc(s_used.sem, 1)

                    @b.vector
                    def _(v):
                        v.sem_inc(s_added.sem, 4)

                        def prepare(i, h):
                            build_hot(v, hot[h][:], i * 16 + 8 * h).then_inc(s_hot.sem, 1)
                            s_ld[h].wait(v, i * 16 + 16)
                            v.tensor_tensor(msgs[h][:, :, 0:D].rearrange("p s (h d) -> p s h d", h=HEADS),
                                            raws[h][:].rearrange("p s (h d) -> p s h d", h=HEADS),
                                            weight[:, bass.ds(i * 16 + 8 * h, 8), :].unsqueeze(3).to_broadcast([P, 8, HEADS, HD]),
                                            ALU.mult).then_inc(s_a.sem, 1)

                        with v.Fori(0, TURNS) as i:
                            for h in range(2):
                                s_used.wait(v, i * 16 + 8 * h + 8)
                                prepare(i, h)
                                tiles = load_registers(v, f"m{h}", nrow, i * 16 + 8 * h, 8, NT - 1)
                                for j in range(8 * h, 8 * h + 8):
                                    a_n = acc[:, tiles[j % 8], :]
                                    s_used.wait(v, i * 16 + j + 17)
                                    s_added.wait(v, i * 16 + j + 4)
                                    v.tensor_tensor(a_n, a_n, ps[j % 4][:, 0:ROW], ALU.add).then_inc(s_added.sem, 1)
                s_a.after(2 * TURNS)
                s_act.after(2 * TURNS)
                s_hot.after(2 * TURNS)
                s_used.after(STEPS + 16)
                s_added.after(STEPS + 4)
                s_ld[0].after(16 * TURNS)
                s_ld[1].after(16 * TURNS)

                with nc.Block() as b:
                    @b.vector
                    def _(v):
                        c = Chain(v, s_dve)
                        den, num = acc[:, :, D:ROW], acc[:, :, 0:D]
                        c.step(v.tensor_scalar(den, den, 1e-12, None, ALU.add))
                        c.step(v.reciprocal(den, den))
                        nh = num.rearrange("p n (h d) -> p n h d", h=HEADS)
                        c.step(v.tensor_tensor(nh, nh, den.unsqueeze(3).to_broadcast([P, NT, HEADS, HD]), ALU.mult))
                        c.step(v.tensor_tensor(xs[:], xs[:], num, ALU.add))
                s_dve.after(4)
        row_statistics()
        finish_statistics()

        with ExitStack() as ph:
            FC = FF // P
            tt = sb("v_t", [P, KD, NPAD], F32, ph)
            w1 = [sb(f"f_w1s{k}", [P, KD, FF], F32, ph) for k in range(2)]
            w2 = [sb(f"f_w2s{k}", [P, FC, D], F32, ph) for k in range(2)]
            b1 = [sb(f"f_b1s{k}", [P, FC], F32, ph) for k in range(2)]
            b2 = [sb(f"f_b2s{k}", [P, D], F32, ph) for k in range(2)]
            gamma = sb("gamma", [P, D], F32, ph)
            beta = sb("beta", [P, D], F32, ph)
            wr = sb("f_wrs", [P, KD, EXPERTS], F32, ph)
            br = sb("f_brs", [1, EXPERTS], F32, ph)
            vmean = sb("vmean", [P, KD], F32, ph)
            prob = sb("f_prob", [1, 1, EXPERTS], F32, ph)
            load = sb("f_load", [1, 1, EXPERTS], F32, ph)
            one1, one2, tmp8 = (sb(f"f_{k}", [1, 1, EXPERTS], F32, ph) for k in ("one1", "one2", "tmp8"))
            top = sb("f_top", [1, 2], F32, ph)
            sel = sb("f_sel", [1, 2], F32, ph)
            sel_i = sb("f_seli", [1, 4], I32, ph)
            total = sb("f_total", [1, 1], F32, ph)
            wsel = sb("f_wsel", [P, 2], F32, ph)
            xn = [sb(f"f_xn{k}", [P, D], F32, ph) for k in range(2)]
            with nc.Block() as b:
                @b.sync
                def _(sp):
                    sp.dma_start(wr[:], f_wr.rearrange("(k p) e -> p k e", p=P)).then_inc(s_in.sem, 16)
                    sp.dma_start(br[:], f_br).then_inc(s_in.sem, 16)
                    sp.dma_start(gamma[:], f_gamma.to_broadcast([P, D])).then_inc(s_in.sem, 16)
                    sp.dma_start(beta[:], f_beta.to_broadcast([P, D])).then_inc(s_in.sem, 16)
                    s_in.wait(sp, 64)

                @b.vector
                def _(v):
                    with v.Fori(0, NG) as i:
                        for j in range(GT):
                            n = i * GT + j
                            s_a.wait(v, i * GT + max(j - 1, 0))
                            v.tensor_scalar(xn[j % 2][:], xs[:, n, :], mean[:, bass.ds(n, 1)], rstd[:, bass.ds(n, 1)],
                                            ALU.subtract, ALU.mult).then_inc(s_dve.sem, 1)

                @b.tensor
                def _(t):
                    with t.Fori(0, NG) as i:
                        for j in range(GT):
                            s_dve.wait(t, i * GT + j + 1)
                            s_act.wait(t, i * GT + max(j - 3, 0))
                            for k in range(KD):
                                m = t.transpose(ps[j % 4][:, k * P:(k + 1) * P], xn[j % 2][:, k * P:(k + 1) * P], ident[:])
                            m.then_inc(s_a.sem, 1)

                @b.scalar
                def _(a):
                    with a.Fori(0, NG) as i:
                        for j in range(GT):
                            s_a.wait(a, i * GT + j + 1)
                            a.copy(tt[:, :, bass.ds((i * GT + j) * P, P)],
                                   ps[j % 4][:, 0:D].rearrange("p (k c) -> p k c", k=KD)).then_inc(s_act.sem, 1)
            s_in.after(64)
            for s in (s_dve, s_a, s_act):
                s.after(NT)

            vector_steps = []
            with nc.Block() as b:
                @b.vector
                def _(v):
                    c = Chain(v, s_dve)
                    c.step(v.tensor_reduce(vmean[:], tt[:, :, 0:NODES], AX, ALU.add))
                    c.did(v.tensor_scalar(vmean[:], vmean[:], 1.0 / NODES, None, ALU.mult))
                    s_pe.wait(v, 1)
                    pr, ld = prob[:], load[:]
                    c.step(v.tensor_tensor(pr[:, 0, :], ps[0][0:1, 0:EXPERTS], br[:], ALU.add))

                    def softmax(x, nth):
                        c.step(v.tensor_reduce(total[:], x, AX, ALU.max))
                        c.step(v.tensor_scalar(x, x, total[:, 0:1], None, ALU.subtract))
                        v.sem_inc(s_b.sem, 1)
                        s_act.wait(v, nth)
                        c.step(v.tensor_reduce(total[:], x, AX, ALU.add))
                        c.step(v.reciprocal(total[:], total[:]))
                        c.step(v.tensor_scalar(x, x, total[:, 0:1], None, ALU.mult))

                    softmax(pr[:, 0, :], 1)
                    c.step(v.tensor_scalar(ld, pr, float(NODES), None, ALU.mult))
                    c.step(v.reciprocal(ld, ld))
                    c.step(v.tensor_scalar(ld, ld, CAPACITY, 1.0, ALU.mult, ALU.min))
                    c.step(v.tensor_tensor(pr, pr, ld, ALU.mult))
                    softmax(pr[:, 0, :], 2)
                    first_two(c, pr, iota8m[0:1, :].unsqueeze(1), one1[:], one2[:], top[:, 0:1], top[:, 1:2],
                              sel[:, 0:1], sel[:, 1:2], tmp8[:], 1)
                    c.step(v.tensor_scalar(sel[:], sel[:], float(EXPERTS), None, ALU.add))
                    c.step(v.tensor_copy(sel_i[:, 0:2], sel[:]))
                    v.sem_inc(s_c.sem, 1)
                    softmax(top[:], 3)
                    v.sem_inc(s_d.sem, 1)
                    s_pe.wait(v, 2)
                    c.step(v.tensor_copy(wsel[:], ps[1][:, 0:2]))
                    s_in.wait(v, 16 * 8)
                    c.step(v.tensor_scalar(b2[0][:], b2[0][:], wsel[:, 0:1], None, ALU.mult))
                    c.step(v.scalar_tensor_tensor(b2[0][:], b2[1][:], wsel[:, 1:2], b2[0][:], ALU.mult, ALU.add))
                    vector_steps.append(c.n)

                @b.scalar
                def _(a):
                    for k, x in enumerate((prob[:, 0, :], prob[:, 0, :], top[:])):
                        s_b.wait(a, k + 1)
                        a.activation(x, x, ACT.Exp).then_inc(s_act.sem, 1)

                @b.tensor
                def _(t):
                    s_dve.wait(t, 2)
                    for k in range(KD):
                        m = t.matmul(ps[0][0:1, 0:EXPERTS], vmean[:, k:k + 1], wr[:, k, :], start=(k == 0), stop=(k == KD - 1))
                    m.then_inc(s_pe.sem, 1)
                    s_d.wait(t, 1)
                    t.matmul(ps[1][:, 0:2], ones[0:1, :], top[:], start=True, stop=True).then_inc(s_pe.sem, 1)

                @b.sync
                def _(sp):
                    s_c.wait(sp, 1)
                    chosen = load_registers(sp, "expert", sel_i, 0, 2, EXPERTS - 1)
                    for k, e in enumerate(chosen):
                        sp.dma_start(w1[k][:], f_w1[e].rearrange("(k p) f -> p k f", p=P)).then_inc(s_in.sem, 16)
                        sp.dma_start(w2[k][:], f_w2[e].rearrange("(k p) f -> p k f", p=P)).then_inc(s_in.sem, 16)
                        sp.dma_start(b1[k][:], f_b1[e]).then_inc(s_in.sem, 16)
                        sp.dma_start(b2[k][:], f_b2[e].to_broadcast([P, D])).then_inc(s_in.sem, 16)
                    s_in.wait(sp, 16 * 8)
            s_in.after(16 * 8)
            s_dve.after(vector_steps[0])
            s_act.after(3)
            s_b.after(3)
            s_c.after(1)
            s_d.after(1)
            s_pe.after(2)

            UE = 2 * FC
            hid = [sb(f"f_hid{k}", [P, FC, GT * P], F32, ph) for k in range(1)]
            ov = sb("f_ov", [P, GT, D], F32, ph)
            vbn = sb("f_vbn", [P, GT, 6], F32, ph)
            vm, vr, vt = (sb(f"f_v{k}", [P, GT], F32, ph) for k in "mrt")
            res = sb("f_res", [P, GT, D], F32, ph)
            with nc.Block() as b:
                @b.tensor
                def _(t):
                    with t.Fori(0, NG) as i:
                        for e in range(2):
                            for u in range(UE):
                                f, q = divmod(u, 2)
                                s_act.wait(t, i * (2 * UE) + max(UE * e + u - 3, 0))
                                for k in range(KD):
                                    m = t.matmul(ps[u % 4][:, 0:GH], w1[e][:, k, f * P:(f + 1) * P],
                                                 tt[:, k, bass.ds(i * (GT * P) + q * GH, GH)], start=(k == 0), stop=(k == KD - 1))
                                m.then_inc(s_a.sem, 1)
                            s_act.wait(t, i * (2 * UE) + UE * (e + 1))
                            for j in range(GT):
                                item = GT * e + j
                                s_b.wait(t, i * (2 * GT) + max(item - 3, 0))
                                for k in range(FC):
                                    m = t.matmul(ps[4 + item % 4][:, 0:D], hid[0][:, k, j * P:(j + 1) * P], w2[e][:, k, :],
                                                 start=(k == 0), stop=(k == FC - 1))
                                m.then_inc(s_c.sem, 1)

                @b.scalar
                def _(a):
                    with a.Fori(0, NG) as i:
                        for e in range(2):
                            for u in range(UE):
                                f, q = divmod(u, 2)
                                s_a.wait(a, i * (2 * UE) + UE * e + u + 1)
                                if u == 0:
                                    s_c.wait(a, i * (2 * GT) + GT * e)
                                a.activation(hid[0][:, f, q * GH:(q + 1) * GH], ps[u % 4][:, 0:GH], ACT.Gelu,
                                             bias=b1[e][:, f:f + 1]).then_inc(s_act.sem, 1)
                        s_d.wait(a, i + 1)
                        a.activation(vr[:], vr[:], ACT.Sqrt).then_inc(s_e.sem, 1)

                chain_steps = 3 * GT + 12

                @b.vector
                def _(v):
                    with v.Fori(0, NG) as i:
                        c = Chain(v, s_dve, i * chain_steps)
                        for j in range(GT):
                            n = i * GT + j
                            c.did(v.tensor_scalar(ov[:, j, :], xs[:, n, :], mean[:, bass.ds(n, 1)], rstd[:, bass.ds(n, 1)],
                                                  ALU.subtract, ALU.mult))
                        c.hold()
                        c.step(v.tensor_tensor(ov[:], ov[:], b2[0][:].unsqueeze(1).to_broadcast([P, GT, D]), ALU.add))
                        for item in range(2 * GT):
                            e, j = divmod(item, GT)
                            s_c.wait(v, i * (2 * GT) + item + 1)
                            if e:
                                s_b.wait(v, i * (2 * GT) + item - GT + 1)
                            v.scalar_tensor_tensor(ov[:, j, :], ps[4 + item % 4][:, 0:D], wsel[:, e:e + 1], ov[:, j, :],
                                                   ALU.mult, ALU.add).then_inc(s_b.sem, 1)
                        s_b.wait(v, i * (2 * GT) + 2 * GT)
                        for j in range(GT):
                            c.did(v.bn_stats(vbn[:, j, :], ov[:, j, :]))
                        c.hold()
                        me, mo, ve, vo = (vbn[:, :, k] for k in (1, 4, 2, 5))
                        c.did(v.tensor_tensor(vm[:], me, mo, ALU.add))
                        c.did(v.tensor_tensor(vt[:], me, mo, ALU.subtract))
                        c.did(v.tensor_tensor(vr[:], ve, vo, ALU.add))
                        c.hold()
                        c.did(v.tensor_scalar(vm[:], vm[:], 0.5, None, ALU.mult))
                        c.step(v.tensor_tensor(vt[:], vt[:], vt[:], ALU.mult))
                        c.step(v.scalar_tensor_tensor(vr[:], vt[:], D / 4.0, vr[:], ALU.mult, ALU.add))
                        c.step(v.tensor_scalar(vr[:], vr[:], 1.0 / D, EPS, ALU.mult, ALU.add))
                        v.sem_inc(s_d.sem, 1)
                        s_e.wait(v, i + 1)
                        c.step(v.reciprocal(vr[:], vr[:]))
                        s_out.wait(v, i * 16)
                        for j in range(GT):
                            c.did(v.tensor_scalar(ov[:, j, :], ov[:, j, :], vm[:, j:j + 1], vr[:, j:j + 1], ALU.subtract, ALU.mult))
                        c.hold()
                        wide = [P, GT, D]
                        c.step(v.tensor_tensor(ov[:], ov[:], gamma[:].unsqueeze(1).to_broadcast(wide), ALU.mult))
                        c.step(v.tensor_tensor(ov[:], ov[:], beta[:].unsqueeze(1).to_broadcast(wide), ALU.add))
                        c.step(v.tensor_tensor(res[:], ov[:], xs[:, bass.ds(i * GT, GT), :], ALU.add))
                        assert c.n == chain_steps
                        v.sem_inc(s_f.sem, 1)

                @b.sync
                def _(sp):
                    view = out.rearrange("(g n p) f -> g p n f", p=P, n=GT)
                    with sp.Fori(0, NG) as i:
                        s_f.wait(sp, i + 1)
                        sp.dma_start(view[i], res[:]).then_inc(s_out.sem, 16)
                    s_out.wait(sp, 16 * NG)
            s_out.after(16 * NG)


def kernel(x, src, dst, edge_type_8, L0_gnn_W1, L0_gnn_b1, L0_gnn_W2, L0_gnn_b2, L0_ffn_router_w,
           L0_ffn_w1, L0_ffn_b1, L0_ffn_w2, L0_ffn_b2, L1_gnn_W, L1_gnn_attn_src, L1_gnn_attn_dst,
           L1_ffn_Wr, L1_ffn_br, L1_ffn_W1, L1_ffn_b1, L1_ffn_W2, L1_ffn_b2, L1_ffn_gamma, L1_ffn_beta):
    import numpy as np
    import concourse.bacc as bacc
    from concourse.bass_utils import run_bass_kernel_spmd

    def tiles(a, fill):
        a = np.asarray(a)
        full = np.full((ETP * P,), fill, a.dtype)
        full[:EDGES] = a
        return full.reshape(ETP, P)

    x = np.asarray(x)
    x_full = np.zeros((NPAD, D), x.dtype)
    x_full[:NODES] = x
    dst_t = tiles(dst, PAD_DST)
    arrays = {
        "x": x_full,
        "src": tiles(src, 0),
        "dst": dst_t,
        "typ": tiles(edge_type_8, 0),
        "dst_e": dst_t.T,
        "dst_first": dst_t[:, 0][None],
        "g_w1": L0_gnn_W1, "g_b1": np.asarray(L0_gnn_b1)[None], "g_w2": L0_gnn_W2, "g_b2": np.asarray(L0_gnn_b2)[None],
        "m_rw": np.asarray(L0_ffn_router_w).T,
        "m_w1": L0_ffn_w1,
        "m_b1": np.asarray(L0_ffn_b1).reshape(EXPERTS, KD, P).transpose(2, 0, 1),
        "m_w2": L0_ffn_w2, "m_b2": L0_ffn_b2,
        "a_w": L1_gnn_W,
        "a_wt": np.asarray(L1_gnn_W).transpose(2, 0, 1),
        "a_src": np.asarray(L1_gnn_attn_src)[:, :, None], "a_dst": np.asarray(L1_gnn_attn_dst)[:, :, None],
        "f_wr": L1_ffn_Wr, "f_br": np.asarray(L1_ffn_br)[None],
        "f_w1": L1_ffn_W1,
        "f_b1": np.asarray(L1_ffn_b1).reshape(EXPERTS, FF // P, P).transpose(0, 2, 1),
        "f_w2": L1_ffn_W2, "f_b2": np.asarray(L1_ffn_b2)[:, None, :],
        "f_gamma": np.asarray(L1_ffn_gamma)[None], "f_beta": np.asarray(L1_ffn_beta)[None],
    }
    nc = bacc.Bacc("TRN2", target_bir_lowering=False, num_devices=1)
    feeds, args = {}, []
    for name, a in arrays.items():
        a = np.ascontiguousarray(a)
        feeds[f"in_{name}"] = a
        args.append(nc.dram_tensor(f"in_{name}", a.shape, mybir.dt.from_np(a.dtype), kind="ExternalInput").ap())
    out = nc.dram_tensor("out", (NPAD, D), F32, kind="ExternalOutput").ap()
    gnn_ffn_kernel(nc, *args, out)
    r = run_bass_kernel_spmd(nc, [feeds], core_ids=[0])
    return r.results[0]["out"][:NODES]
```

```python
from contextlib import ExitStack

import concourse.bass as bass
from concourse import mybir

ALU = mybir.AluOpType
ACT = mybir.ActivationFunctionType
F32 = mybir.dt.float32
BF16 = mybir.dt.bfloat16
I32 = mybir.dt.int32
AX = mybir.AxisListType.X

P = 128
NODES = 6250
D = 256
KD = D // P
HID = 128
EDGES = 100000
TYPES = 8
HEADS = 8
HD = D // HEADS
EXPERTS = 8
FF = 512
NT = -(-NODES // P)
NPAD = NT * P
ET = -(-EDGES // P)
STEPS = -(-(ET + NT - 1) // 16) * 16
ETP = ET + 2
SCH = -(-(STEPS + 8) // P)
PSTEPS = SCH * P
TURNS = STEPS // 16
PAD_DST = 1 << 20
ROW = D + HEADS
GT = 7
NG = NT // GT
GH = GT * P // 2
CH = P // HEADS
CS = STEPS // CH
CW = CS * P
EPS = 1e-5
CAPACITY = float(-(-NODES * 5 // (4 * EXPERTS)))


class Signal:

    def __init__(self, ctx, nc, name):
        self.sem = ctx.enter_context(nc.semaphore(name))
        self.base = 0

    def lift(self, engine):
        engine.sem_inc(self.sem, 1)
        self.base = 1

    def wait(self, engine, n):
        engine.wait_ge(self.sem, n + self.base)
        if engine.engine in (mybir.EngineType.SP, mybir.EngineType.Pool) and not isinstance(n, int):
            engine.nop(nofuse=True)

    def after(self, n):
        self.base += n


class Chain:

    def __init__(self, engine, counts, start=0):
        self.engine, self.counts, self.start, self.n = engine, counts, start, 0

    def did(self, instruction):
        instruction.then_inc(self.counts.sem, 1)
        self.n += 1

    def hold(self):
        self.counts.wait(self.engine, self.start + self.n)

    def step(self, instruction):
        self.did(instruction)
        self.hold()


def load_registers(engine, name, row, start, count, top):
    regs = [engine.alloc_register(f"{name}_{engine.engine.name}_{q}") for q in range(count)]
    engine.load(regs, row[0:1, bass.ds(start, count)])
    return [engine.snap(r, min_val=0, max_val=top) for r in regs]


def first_two(c, prob, iota8m, one1, one2, top1, top2, idx1, idx2, tmp, n):
    v = c.engine
    shape = [prob.shape[0], n, 8]

    def wide(x):
        return x.unsqueeze(2).to_broadcast(shape)

    def pick(src, top, idx, one):
        c.step(v.tensor_reduce(top, src, AX, ALU.max))
        c.step(v.tensor_tensor(tmp, src, wide(top), ALU.is_equal))
        c.step(v.tensor_tensor(tmp, tmp, iota8m, ALU.mult))
        c.step(v.tensor_reduce(idx, tmp, AX, ALU.min))
        c.step(v.tensor_tensor(one, iota8m, wide(idx), ALU.is_equal))

    pick(prob, top1, idx1, one1)
    c.step(v.scalar_tensor_tensor(one2, one1, -4.0, prob, ALU.mult, ALU.add))
    pick(one2, top2, idx2, one2)


def gnn_ffn_kernel(nc, x, src, dst, typ, dst_e, dst_first, g_w1, g_b1, g_w2, g_b2, m_rw, m_w1, m_b1,
                   m_w2, m_b2, a_w, a_wt, a_src, a_dst, f_wr, f_br, f_w1, f_b1, f_w2, f_b2, f_gamma,
                   f_beta, out):
    ctx = ExitStack()

    def sb(name, shape, dt=F32, where=ctx):
        return where.enter_context(nc.sbuf_tensor(name, shape, dt))

    def sig(name):
        return Signal(ctx, nc, name)

    with ctx:
        t_gcn = [nc.dram_tensor(f"t_gcn{k}", (NPAD, HID), F32, kind="Internal").ap() for k in range(2)]
        t_msg = nc.dram_tensor("t_msg", (NPAD * TYPES, ROW), F32, kind="Internal").ap()
        t_path = nc.dram_tensor("t_path", (STEPS // 8, P, 8 * D), F32, kind="Internal").ap()

        xs = sb("xs", [P, NT, D])
        idx1 = sb("idx1", [P, PSTEPS], I32)
        idx3 = sb("idx3", [P, PSTEPS], I32)
        dloc = sb("dloc", [P, PSTEPS])
        typf = sb("typf", [P, PSTEPS])
        key = sb("key", [P, PSTEPS])
        nrow = sb("nrow", [1, PSTEPS], I32)
        iota = sb("iota", [P, P])
        ident = sb("ident", [P, P])
        iota8m = sb("iota8m", [P, 8])
        ones = sb("ones", [1, P])
        dinv = sb("dinv", [P, NT])
        bn6 = sb("bn6", [P, NT, 6])
        mean = sb("mean", [P, NT])
        rstd = sb("rstd", [P, NT])
        lntmp = sb("lntmp", [P, NT])
        stage = sb("stage", [P, 32], I32)
        ps = [ctx.enter_context(nc.psum_tensor(f"ps{b}", [P, 512], F32)) for b in range(8)]

        s_in = sig("s_in")
        s_out = sig("s_out")
        s_pool = sig("s_pool")
        s_dve = sig("s_dve")
        s_act = sig("s_act")
        s_pe = sig("s_pe")
        s_row = [sig(f"s_row{j}") for j in range(32)]
        s_stage = sig("s_stage")
        s_used = sig("s_used")
        s_hot = sig("s_hot")
        s_added = sig("s_added")
        s_ld = [sig(f"s_ld{j}") for j in range(4)]
        s_a, s_b, s_c, s_d, s_e, s_f = (sig(f"s_{k}") for k in "abcdef")

        with nc.Block() as b:
            @b.vector
            def _(v):
                for s in (s_pool, s_dve, s_act, s_pe, s_stage, s_used, s_hot, s_added, s_a, s_b, s_c, s_d, s_e, s_f):
                    s.lift(v)

        def row_statistics(v):
            with v.Fori(0, NG) as i:
                for j in range(GT):
                    v.bn_stats(bn6[:, i * GT + j, :], xs[:, i * GT + j, :])

        deg_bufs = ctx.enter_context(ExitStack())
        lo_f = sb("lo_f", [P, ETP], BF16, deg_bufs)
        hi_f = sb("hi_f", [P, ETP], BF16, deg_bufs)
        iota_b = sb("iota_b", [P, P], BF16, deg_bufs)
        DB = ETP // 16

        with ExitStack() as ph:
            iota_i = sb("iota_i", [P, P], I32, ph)
            pcol_i = sb("pcol_i", [P, 1], I32, ph)
            step_i = sb("step_i", [P, SCH], I32, ph)
            tile_i = sb("tile_i", [1, ETP], I32, ph)
            pcol = sb("pcol", [P, 1], F32, ph)
            stepf = sb("stepf", [P, SCH], F32, ph)
            krow = sb("krow", [1, ETP], F32, ph)
            first_i = sb("first_i", [1, ETP], I32, ph)
            kall = sb("kall", [P, ETP], F32, ph)
            kcmp = sb("kcmp", [P, SCH, ETP], F32, ph)
            tf = sb("tf", [P, SCH], F32, ph)
            ti = sb("ti", [P, SCH], I32, ph)
            nf = sb("nf", [P, SCH], F32, ph)
            n128 = sb("n128", [P, SCH], F32, ph)
            raw = [[sb(f"raw{k}_{c}", [P, P], I32, ph) for c in range(SCH)] for k in range(3)]
            rowf = [[sb(f"rowf{k}_{c}", [P, P], F32, ph) for c in range(2)] for k in range(5)]
            lo_i = sb("lo_i", [P, ETP], I32, ph)
            hi_i = sb("hi_i", [P, ETP], I32, ph)
            vector_steps = []

            with nc.Block() as b:
                @b.sync
                def _(sp):
                    sp.dma_start(first_i[:], dst_first).then_inc(s_in.sem, 16)
                    sp.dma_start(lo_i[:], dst_e).then_inc(s_ld[0].sem, 16)
                    s_ld[0].wait(sp, 16)
                    sp.dma_start(hi_i[:], dst_e).then_inc(s_ld[0].sem, 16)
                    xr = x.rearrange("(n p) f -> p n f", p=P)
                    for g in range(NG):
                        sp.dma_start(xs[:, g * GT:(g + 1) * GT, :], xr[:, g * GT:(g + 1) * GT, :]).then_inc(s_ld[1].sem, 16)
                    s_ld[1].wait(sp, 16 * NG)

                @b.gpsimd
                def _(g):
                    g.iota(iota_i[:], [[1, P]], base=0, channel_multiplier=0).then_inc(s_pool.sem, 1)
                    g.iota(pcol_i[:], [[0, 1]], base=0, channel_multiplier=1).then_inc(s_pool.sem, 1)
                    g.iota(step_i[:], [[P, SCH]], base=0, channel_multiplier=1).then_inc(s_pool.sem, 1)
                    g.iota(tile_i[:], [[1, ETP]], base=0, channel_multiplier=0).then_inc(s_pool.sem, 1)
                    s_c.wait(g, 1)
                    for c in range(SCH):
                        for k, a in enumerate((dst, src, typ)):
                            g.indirect_dma_start(out=raw[k][c][:], out_offset=None, in_=a,
                                                 in_offset=bass.IndirectOffsetOnAxis(ap=ti[:, c:c + 1], axis=0)
                                                 ).then_inc(s_row[c].sem, 16)

                @b.vector
                def _(v):
                    c = Chain(v, s_dve)
                    s_pool.wait(v, 4)
                    c.did(v.tensor_copy(iota[:], iota_i[:]))
                    c.did(v.tensor_copy(pcol[:], pcol_i[:]))
                    c.did(v.tensor_copy(stepf[:], step_i[:]))
                    c.did(v.tensor_copy(krow[:], tile_i[:]))
                    c.did(v.memset(ones[:], 1.0))
                    s_in.wait(v, 16)
                    c.step(v.tensor_scalar(first_i[:], first_i[:], 7, None, ALU.arith_shift_right))
                    c.did(v.tensor_scalar(ident[:], iota[:], pcol[:, 0:1], None, ALU.is_equal))
                    c.did(v.tensor_scalar(iota8m[:], iota[:, 0:8], -8.0, None, ALU.add))
                    c.step(v.tensor_scalar(first_i[:], first_i[:], float(NT - 1), None, ALU.min))
                    c.step(v.tensor_tensor(krow[:], krow[:], first_i[:], ALU.add))
                    s_pe.wait(v, 1)
                    c.did(v.tensor_copy(kall[:, 0:392], ps[0][:, 0:392]))
                    c.step(v.tensor_copy(kall[:, 392:ETP], ps[1][:, 0:ETP - 392]))
                    for k in range(SCH):
                        c.did(v.tensor_scalar(kcmp[:, k, :], kall[:], stepf[:, k:k + 1], None, ALU.is_le))
                    c.hold()
                    c.step(v.tensor_reduce(tf[:], kcmp[:, :, 1:ETP], AX, ALU.add))
                    c.did(v.tensor_tensor(nf[:], stepf[:], tf[:], ALU.subtract))
                    c.step(v.tensor_copy(ti[:], tf[:]))
                    v.tensor_scalar(n128[:], nf[:], -float(P), None, ALU.mult).then_inc(s_c.sem, 1)
                    s_c.wait(v, 1)
                    s_ld[1].wait(v, 16 * NG)
                    row_statistics(v)
                    for k in range(SCH):
                        s_row[k].wait(v, 48)
                        if k >= 2:
                            s_act.wait(v, k - 1)
                        r, q = [raw[m][k][:] for m in range(3)], [rowf[m][k % 2][:] for m in range(5)]
                        c.did(v.tensor_scalar(q[0], r[0], n128[:, k:k + 1], None, ALU.add))
                        c.did(v.tensor_copy(q[1], r[0]))
                        c.did(v.tensor_copy(q[2], r[1]))
                        c.did(v.tensor_copy(q[3], r[2]))
                        c.did(v.scalar_tensor_tensor(q[4], r[1], float(TYPES), r[2], ALU.mult, ALU.add))
                        c.hold()
                        v.sem_inc(s_d.sem, 1)
                    s_ld[0].wait(v, 32)
                    c.did(v.tensor_scalar(lo_i[:], lo_i[:], P - 1, None, ALU.bitwise_and))
                    c.step(v.tensor_scalar(hi_i[:], hi_i[:], 7, None, ALU.arith_shift_right))
                    c.did(v.tensor_copy(iota_b[:], iota[:]))
                    c.did(v.tensor_copy(lo_f[:], lo_i[:]))
                    c.did(v.tensor_copy(hi_f[:], hi_i[:]))
                    c.hold()
                    vector_steps.append(c.n)

                @b.tensor
                def _(t):
                    s_dve.wait(t, 10)
                    t.matmul(ps[0][:, 0:392], ones[0:1, :], krow[0:1, 0:392], start=True, stop=True)
                    t.matmul(ps[1][:, 0:ETP - 392], ones[0:1, :], krow[0:1, 392:ETP], start=True, stop=True).then_inc(s_pe.sem, 1)
                    for k in range(SCH):
                        s_d.wait(t, k + 1)
                        if k >= 1:
                            s_act.wait(t, k)
                        for m in range(4):
                            t.transpose(ps[2][:, m * P:(m + 1) * P], rowf[m][k % 2][:], ident[:])
                        t.transpose(ps[3][:, 0:P], rowf[4][k % 2][:], ident[:])
                        t.transpose(ps[3][0:1, P:2 * P], nf[:, k:k + 1], ident[:]).then_inc(s_pe.sem, 1)

                @b.scalar
                def _(a):
                    for k in range(SCH):
                        s_pe.wait(a, k + 2)
                        w = slice(k * P, (k + 1) * P)
                        for m, o in enumerate((dloc, key, idx1, typf)):
                            a.copy(o[:, w], ps[2][:, m * P:(m + 1) * P]).then_inc(s_e.sem, 1)
                        a.copy(idx3[:, w], ps[3][:, 0:P]).then_inc(s_e.sem, 1)
                        a.copy(nrow[:, w], ps[3][0:1, P:2 * P]).then_inc(s_e.sem, 1)
                        s_e.wait(a, 6 * (k + 1))
                        a.sem_inc(s_act.sem, 1)
            s_dve.after(vector_steps[0])
            s_pool.after(4)
            s_in.after(16)
            s_ld[0].after(32)
            s_ld[1].after(16 * NG)
            s_c.after(1)
            s_d.after(SCH)
            s_e.after(6 * SCH)
            s_pe.after(1 + SCH)
            s_act.after(SCH)
            for k in range(SCH):
                s_row[k].after(48)

        def finish_statistics():
            with nc.Block() as b:
                @b.vector
                def _(v):
                    c = Chain(v, s_dve)
                    me, mo, ve, vo = (bn6[:, :, k] for k in (1, 4, 2, 5))
                    c.did(v.tensor_tensor(mean[:], me, mo, ALU.add))
                    c.did(v.tensor_tensor(lntmp[:], me, mo, ALU.subtract))
                    c.did(v.tensor_tensor(rstd[:], ve, vo, ALU.add))
                    c.hold()
                    c.did(v.tensor_scalar(mean[:], mean[:], 0.5, None, ALU.mult))
                    c.step(v.tensor_tensor(lntmp[:], lntmp[:], lntmp[:], ALU.mult))
                    c.step(v.scalar_tensor_tensor(rstd[:], lntmp[:], D / 4.0, rstd[:], ALU.mult, ALU.add))
                    c.step(v.tensor_scalar(rstd[:], rstd[:], 1.0 / D, EPS, ALU.mult, ALU.add))
                    s_act.wait(v, 1)
                    c.did(v.reciprocal(rstd[:], rstd[:]))
                    c.hold()
                    v.drain()

                @b.scalar
                def _(a):
                    s_dve.wait(a, 7)
                    a.activation(rstd[:], rstd[:], ACT.Sqrt).then_inc(s_act.sem, 1)
            s_dve.after(8)
            s_act.after(1)

        def gather_turns(table, slots, idx, halves=2):
            turn = 8 * halves

            def pool(g, free):
                with g.Fori(0, STEPS // turn) as i:
                    for h in range(halves):
                        s_stage.wait(g, i * halves + h + 1)
                        free(g, i, h)
                        for j in range(8 * h, 8 * h + 8):
                            g.indirect_dma_start(out=slots(j), out_offset=None, in_=table,
                                                 in_offset=bass.IndirectOffsetOnAxis(ap=stage[:, j:j + 1], axis=0)
                                                 ).then_inc(s_row[j].sem, 16)

            def act(a, free, i, h):
                free(a, i, h)
                a.copy(stage[:, 8 * h:8 * h + 8], idx[:, bass.ds(i * turn + 8 * h, 8)]).then_inc(s_stage.sem, 1)

            return pool, act

        def after_gathers(halves=2):
            s_stage.after(STEPS // 8)
            for j in range(8 * halves):
                s_row[j].after(16 * (STEPS // (8 * halves)))

        def build_hot(v, buf, start):
            return v.tensor_tensor(buf, dloc[:, bass.ds(start, 8)].unsqueeze(2).to_broadcast([P, 8, P]),
                                   iota[:].unsqueeze(1).to_broadcast([P, 8, P]), ALU.is_equal)

        with ExitStack() as ph:
            acc = sb("acc", [P, NT, HID], F32, ph)
            ring = sb("ring", [P, 16, HID], F32, ph)
            hot = [sb(f"hot{k}", [P, 8, P], F32, ph) for k in range(2)]
            w1 = sb("w1", [P, KD, HID], F32, ph)
            w2 = sb("w2", [P, D], F32, ph)
            b1 = sb("b1", [P, HID], F32, ph)
            xn = [sb(f"xn{k}", [P, D], F32, ph) for k in range(4)]
            xnt = [sb(f"xnt{k}", [P, D], F32, ph) for k in range(4)]

            finish_statistics()

            with ExitStack() as dg:
                deg = sb("deg", [P, NT], F32, dg)
                hot_lo = [sb(f"hot_lo{k}", [P, 16, P], BF16, dg) for k in range(2)]
                hot_hi = [sb(f"hot_hi{k}", [P, 16, NT], BF16, dg) for k in range(2)]
                b2 = sb("b2", [P, D], F32, dg)
                with nc.Block() as b:
                    @b.sync
                    def _(sp):
                        sp.dma_start(w1[:], g_w1.rearrange("(k p) f -> p k f", p=P)).then_inc(s_in.sem, 16)
                        sp.dma_start(w2[:], g_w2).then_inc(s_in.sem, 16)
                        sp.dma_start(b1[:], g_b1.to_broadcast([P, HID])).then_inc(s_in.sem, 16)
                        sp.dma_start(b2[:], g_b2.to_broadcast([P, D])).then_inc(s_in.sem, 16)
                        s_in.wait(sp, 64)

                    @b.gpsimd
                    def _(g):
                        s_in.wait(g, 64)
                        with g.Fori(0, NG) as i:
                            for j in range(GT):
                                n = i * GT + j
                                s_dve.wait(g, n + 1)
                                g.tensor_tensor(xs[:, n, :], xs[:, n, :], b2[:], ALU.add)

                    @b.vector
                    def _(v):
                        def build(i, j):
                            s_c.wait(v, i * GT + max(j - 1, 0))
                            for hots, digits, width in ((hot_lo, lo_f, P), (hot_hi, hi_f, NT)):
                                v.tensor_tensor(hots[j % 2][:], digits[:, bass.ds((i * GT + j) * 16, 16)].unsqueeze(2).to_broadcast([P, 16, width]),
                                                iota_b[:, 0:width].unsqueeze(1).to_broadcast([P, 16, width]),
                                                ALU.is_equal).then_inc(s_a.sem, 1)
                            s_pe.wait(v, i * GT + max(j - 3, 0))
                            n = i * GT + j
                            v.tensor_scalar(xn[j % 4][:], xs[:, n, :], mean[:, bass.ds(n, 1)], rstd[:, bass.ds(n, 1)],
                                            ALU.subtract, ALU.mult).then_inc(s_dve.sem, 1)

                        v.memset(deg[:], 1.0).then_inc(s_d.sem, 1)
                        with v.Fori(0, NG) as i:
                            for j in range(GT):
                                build(i, j)
                            s_c.wait(v, i * GT + GT)
                            s_d.wait(v, i + 1)
                            v.tensor_tensor(deg[:], deg[:], ps[0][:, 0:NT], ALU.add).then_inc(s_d.sem, 1)

                    @b.tensor
                    def _(t):
                        s_in.wait(t, 64)
                        with t.Fori(0, NG) as i:
                            def counts_and_turn(j):
                                s_a.wait(t, i * (2 * GT) + 2 * j + 2)
                                if j == 0:
                                    s_d.wait(t, i + 1)
                                for k in range(16):
                                    m = t.matmul(ps[0][:, 0:NT], hot_lo[j % 2][:, k, :], hot_hi[j % 2][:, k, :],
                                                 start=(j == 0 and k == 0), stop=(j == GT - 1 and k == 15))
                                m.then_inc(s_c.sem, 1)
                                s_dve.wait(t, i * GT + j + 1)
                                s_b.wait(t, i * GT + max(j - 2, 0))
                                for k in range(KD):
                                    m = t.transpose(ps[1 + j % 3][:, k * P:(k + 1) * P], xn[j % 4][:, k * P:(k + 1) * P], ident[:])
                                m.then_inc(s_pe.sem, 1)

                            def project(j):
                                s_b.wait(t, i * GT + j + 1)
                                s_e.wait(t, i * GT + max(j - 3, 0))
                                for k in range(KD):
                                    m = t.matmul(ps[4 + j % 4][:, 0:HID], xnt[j % 4][:, k * P:(k + 1) * P], w1[:, k, :],
                                                 start=(k == 0), stop=(k == KD - 1))
                                m.then_inc(s_f.sem, 1)

                            for j in range(GT + 2):
                                if j < GT:
                                    counts_and_turn(j)
                                if j >= 2:
                                    project(j - 2)

                    @b.scalar
                    def _(a):
                        with a.Fori(0, NG) as i:
                            for j in range(GT + 2):
                                if j < GT:
                                    s_pe.wait(a, i * GT + j + 1)
                                    s_f.wait(a, i * GT + max(j - 3, 0))
                                    a.copy(xnt[j % 4][:], ps[1 + j % 3][:, 0:D]).then_inc(s_b.sem, 1)
                                if j >= 2:
                                    s_f.wait(a, i * GT + j - 1)
                                    a.copy(acc[:, i * GT + j - 2, :], ps[4 + (j - 2) % 4][:, 0:HID]).then_inc(s_e.sem, 1)
                s_in.after(64)
                s_a.after(2 * NT)
                s_d.after(1 + NG)
                for s in (s_b, s_c, s_e, s_f, s_pe, s_dve):
                    s.after(NT)

                with nc.Block() as b:
                    @b.scalar
                    def _(a):
                        a.activation(deg[:], deg[:], ACT.Sqrt).then_inc(s_act.sem, 1)

                    @b.vector
                    def _(v):
                        c = Chain(v, s_dve)
                        s_act.wait(v, 1)
                        c.step(v.reciprocal(dinv[:], deg[:]))
                        c.step(v.tensor_tensor(acc[:], acc[:], dinv[:].unsqueeze(2).to_broadcast([P, NT, HID]), ALU.mult))

                    @b.sync
                    def _(sp):
                        s_dve.wait(sp, 2)
                        sp.dma_start(t_gcn[0].rearrange("(n p) f -> p n f", p=P), acc[:]).then_inc(s_out.sem, 16)
                        s_out.wait(sp, 16)
                s_act.after(1)
                s_dve.after(2)
                s_out.after(16)

            for conv in range(2):
                with nc.Block() as b:
                    pool, stage_half = gather_turns(t_gcn[conv], lambda j: ring[:, j, :], idx1)

                    def rows_used(engine, i, h):
                        s_used.wait(engine, i * 16 + 8 * h + 8)

                    @b.gpsimd
                    def _(g):
                        pool(g, rows_used)

                    @b.scalar
                    def _(a):
                        with a.Fori(0, TURNS) as i:
                            for h in range(2):
                                stage_half(a, rows_used, i, h)

                    @b.tensor
                    def _(t):
                        t.sem_inc(s_used.sem, 16)
                        with t.Fori(0, TURNS) as i:
                            for h in range(2):
                                s_hot.wait(t, i * 2 + h + 1)
                                for j in range(8 * h, 8 * h + 8):
                                    s_row[j].wait(t, i * 16 + 16)
                                    s_added.wait(t, i * 16 + j + 1)
                                    t.matmul(ps[j % 4][:, 0:HID], hot[h][:, j % 8, :], ring[:, j, :],
                                             start=True, stop=True).then_inc(s_used.sem, 1)

                    @b.vector
                    def _(v):
                        v.sem_inc(s_added.sem, 4)
                        build_hot(v, hot[0][:], 0).then_inc(s_hot.sem, 1)
                        with v.Fori(0, TURNS) as i:
                            for h in range(2):
                                s_used.wait(v, i * 16 + 8 * h + 16)
                                build_hot(v, hot[1 - h][:], i * 16 + 8 * h + 8).then_inc(s_hot.sem, 1)
                                tiles = load_registers(v, f"c{conv}h{h}", nrow, i * 16 + 8 * h, 8, NT - 1)
                                for j in range(8 * h, 8 * h + 8):
                                    a_n = acc[:, tiles[j % 8], :]
                                    s_used.wait(v, i * 16 + j + 17)
                                    s_added.wait(v, i * 16 + j + 4)
                                    v.tensor_tensor(a_n, a_n, ps[j % 4][:, 0:HID], ALU.add).then_inc(s_added.sem, 1)
                s_used.after(STEPS + 16)
                s_added.after(STEPS + 4)
                s_hot.after(2 * TURNS + 1)
                after_gathers()
                if conv == 0:
                    with nc.Block() as b:
                        @b.vector
                        def _(v):
                            c = Chain(v, s_dve)
                            wide = [P, NT, HID]
                            dv = dinv[:].unsqueeze(2).to_broadcast(wide)
                            c.step(v.tensor_tensor(acc[:], acc[:], dv, ALU.mult))
                            c.step(v.tensor_tensor(acc[:], acc[:], b1[:].unsqueeze(1).to_broadcast(wide), ALU.add))
                            c.step(v.scalar_tensor_tensor(acc[:], acc[:], 0.0, dv, ALU.max, ALU.mult))

                        @b.sync
                        def _(sp):
                            s_dve.wait(sp, 3)
                            sp.dma_start(t_gcn[1].rearrange("(n p) f -> p n f", p=P), acc[:]).then_inc(s_out.sem, 16)
                            s_out.wait(sp, 16)
                    s_dve.after(3)
                    s_out.after(16)

            with nc.Block() as b:
                @b.vector
                def _(v):
                    with v.Fori(0, NG) as i:
                        for j in range(GT + 3):
                            if j < GT:
                                n = i * GT + j
                                s_pe.wait(v, i * GT + max(j - 3, 0))
                                v.tensor_scalar(xn[j % 4][:, 0:HID], acc[:, n, :], dinv[:, bass.ds(n, 1)], None,
                                                ALU.mult).then_inc(s_a.sem, 1)
                            if j >= 3:
                                n = i * GT + j - 3
                                s_b.wait(v, n + 1)
                                v.tensor_tensor(xs[:, n, :], xs[:, n, :], ps[4 + (j - 3) % 4][:, 0:D], ALU.add).then_inc(s_dve.sem, 1)
                        s_dve.wait(v, i * GT + GT)
                        for j in range(GT):
                            v.bn_stats(bn6[:, i * GT + j, :], xs[:, i * GT + j, :])

                @b.tensor
                def _(t):
                    with t.Fori(0, NG) as i:
                        for j in range(GT + 2):
                            if j < GT:
                                s_a.wait(t, i * GT + j + 1)
                                s_act.wait(t, i * GT + max(j - 3, 0))
                                t.transpose(ps[j % 4][:, 0:P], xn[j % 4][:, 0:HID], ident[:]).then_inc(s_pe.sem, 1)
                            if j >= 2:
                                s_act.wait(t, i * GT + j - 1)
                                s_dve.wait(t, i * GT + max(j - 5, 0))
                                t.matmul(ps[4 + (j - 2) % 4][:, 0:D], xnt[(j - 2) % 4][:, 0:P], w2[:], start=True, stop=True).then_inc(s_b.sem, 1)

                @b.scalar
                def _(a):
                    with a.Fori(0, NG) as i:
                        for j in range(GT):
                            s_pe.wait(a, i * GT + j + 1)
                            s_b.wait(a, i * GT + max(j - 3, 0))
                            a.copy(xnt[j % 4][:, 0:P], ps[j % 4][:, 0:P]).then_inc(s_act.sem, 1)
            for s in (s_a, s_b, s_dve, s_pe, s_act):
                s.after(NT)
        deg_bufs.close()
        finish_statistics()

        with ExitStack() as ph:
            tt = sb("tt", [P, KD, NPAD], F32, ph)
            w1 = sb("m_w1s", [P, EXPERTS, KD, D], F32, ph)
            w2 = sb("m_w2s", [P, EXPERTS, KD, D], F32, ph)
            b1 = sb("m_b1s", [P, EXPERTS, KD], F32, ph)
            b2 = sb("m_b2s", [EXPERTS, D], F32, ph)
            rw = sb("m_rws", [P, KD, EXPERTS], F32, ph)
            prob = sb("prob", [P, NT, EXPERTS], F32, ph)
            one1 = sb("one1", [P, NT, EXPERTS], F32, ph)
            one2 = sb("one2", [P, NT, EXPERTS], F32, ph)
            tmp8 = sb("tmp8", [P, NT, EXPERTS], F32, ph)
            top1, top2, i1, i2 = (sb(f"m_{k}", [P, NT], F32, ph) for k in ("top1", "top2", "i1", "i2"))
            comb, total = prob, i1
            hid = [sb(f"m_hid{k}", [P, KD, GT * P], F32, ph) for k in range(2)]
            xn = [sb(f"m_xn{k}", [P, D], F32, ph) for k in range(4)]
            xnt = [sb(f"m_xnt{k}", [P, D], F32, ph) for k in range(4)]
            cst = sb("m_c", [P, GT, EXPERTS], F32, ph)
            ctt = sb("m_ct", [EXPERTS, GT, P], F32, ph)

            with nc.Block() as b:
                @b.sync
                def _(sp):
                    sp.dma_start(rw[:], m_rw.rearrange("(k p) e -> p k e", p=P)).then_inc(s_in.sem, 16)
                    sp.dma_start(w1[:], m_w1.rearrange("e (k p) f -> p e k f", p=P)).then_inc(s_out.sem, 16)
                    sp.dma_start(w2[:], m_w2.rearrange("e (k p) f -> p e k f", p=P)).then_inc(s_out.sem, 16)
                    sp.dma_start(b1[:], m_b1).then_inc(s_out.sem, 16)
                    sp.dma_start(b2[:], m_b2).then_inc(s_out.sem, 16)
                    s_out.wait(sp, 64)

                LAG = 2

                @b.vector
                def _(v):
                    with v.Fori(0, NG) as i:
                        for j in range(GT + LAG + 1):
                            if j < GT:
                                n = i * GT + j
                                s_a.wait(v, i * GT + max(j - 3, 0))
                                s_d.wait(v, i * GT + max(j - 3, 0))
                                v.tensor_scalar(xn[j % 4][:], xs[:, n, :], mean[:, bass.ds(n, 1)], rstd[:, bass.ds(n, 1)],
                                                ALU.subtract, ALU.mult).then_inc(s_dve.sem, 1)
                                s_dve.wait(v, n + 1)
                                v.tensor_tensor(xs[:, n, :], xs[:, n, :], xn[j % 4][:], ALU.add).then_inc(s_d.sem, 1)
                            if j > LAG:
                                n = i * GT + j - LAG - 1
                                s_c.wait(v, n + 1)
                                v.tensor_copy(prob[:, n, :], ps[4 + (j - LAG - 1) % 4][:, 0:EXPERTS]).then_inc(s_e.sem, 1)

                @b.scalar
                def _(a):
                    with a.Fori(0, NG) as i:
                        for j in range(GT):
                            s_a.wait(a, i * GT + j + 1)
                            s_b.wait(a, i * GT + max(j - 3, 0))
                            s_c.wait(a, i * GT + max(j - 3, 0))
                            a.copy(xnt[j % 4][:], ps[j % 4][:, 0:D]).then_inc(s_act.sem, 1)

                @b.gpsimd
                def _(g):
                    with g.Fori(0, NG) as i:
                        for j in range(GT):
                            s_act.wait(g, i * GT + j + 1)
                            g.tensor_copy(tt[:, :, bass.ds((i * GT + j) * P, P)],
                                          xnt[j % 4][:].rearrange("p (k c) -> p k c", k=KD)).then_inc(s_b.sem, 1)

                @b.tensor
                def _(t):
                    s_in.wait(t, 16)
                    with t.Fori(0, NG) as i:
                        for j in range(GT + LAG):
                            if j < GT:
                                s_dve.wait(t, i * GT + j + 1)
                                s_act.wait(t, i * GT + max(j - 3, 0))
                                for k in range(KD):
                                    m = t.transpose(ps[j % 4][:, k * P:(k + 1) * P], xn[j % 4][:, k * P:(k + 1) * P], ident[:])
                                m.then_inc(s_a.sem, 1)
                            if j >= LAG:
                                q = j - LAG
                                s_act.wait(t, i * GT + q + 1)
                                s_e.wait(t, i * GT + max(q - 3, 0))
                                for k in range(KD):
                                    m = t.matmul(ps[4 + q % 4][:, 0:EXPERTS], xnt[q % 4][:, k * P:(k + 1) * P], rw[:, k, :],
                                                 start=(k == 0), stop=(k == KD - 1))
                                m.then_inc(s_c.sem, 1)
            s_in.after(16)
            s_out.after(64)
            for s in (s_a, s_b, s_c, s_d, s_e, s_dve, s_act):
                s.after(NT)

            with nc.Block() as b:
                vector_steps = []
                wide = [P, NT, EXPERTS]

                @b.vector
                def _(v):
                    c = Chain(v, s_dve)
                    c.step(v.tensor_reduce(top1[:], prob[:], AX, ALU.max))
                    c.step(v.tensor_tensor(prob[:], prob[:], top1[:].unsqueeze(2).to_broadcast(wide), ALU.subtract))
                    s_act.wait(v, 1)
                    c.step(v.tensor_reduce(total[:], prob[:], AX, ALU.add))
                    c.step(v.reciprocal(total[:], total[:]))
                    c.step(v.tensor_tensor(prob[:], prob[:], total[:].unsqueeze(2).to_broadcast(wide), ALU.mult))
                    first_two(c, prob[:], iota8m[:].unsqueeze(1).to_broadcast(wide), one1[:], one2[:], top1[:], top2[:],
                              i1[:], i2[:], tmp8[:], NT)
                    c.step(v.tensor_tensor(total[:], top1[:], top2[:], ALU.add))
                    c.step(v.tensor_scalar(total[:], total[:], 1e-12, None, ALU.max))
                    c.step(v.reciprocal(total[:], total[:]))
                    c.did(v.tensor_tensor(one1[:], one1[:], top1[:].unsqueeze(2).to_broadcast(wide), ALU.mult))
                    c.did(v.tensor_tensor(one2[:], one2[:], top2[:].unsqueeze(2).to_broadcast(wide), ALU.mult))
                    c.hold()
                    c.step(v.tensor_tensor(one1[:], one1[:], one2[:], ALU.add))
                    c.step(v.tensor_tensor(comb[:], one1[:], total[:].unsqueeze(2).to_broadcast(wide), ALU.mult))
                    vector_steps.append(c.n)

                @b.scalar
                def _(a):
                    s_dve.wait(a, 2)
                    a.activation(prob[:], prob[:], ACT.Exp).then_inc(s_act.sem, 1)
            s_dve.after(vector_steps[0])
            s_act.after(1)

            UE = 2 * KD
            ITEMS = GT * (EXPERTS + 1)
            with nc.Block() as b:
                @b.tensor
                def _(t):
                    def up(i, e):
                        for u in range(UE):
                            f, q = divmod(u, 2)
                            s_act.wait(t, i * (UE * EXPERTS) + max(UE * (e - 1) + u + 1, 0))
                            for k in range(KD):
                                m = t.matmul(ps[u][:, 0:GH], w1[:, e, k, f * P:(f + 1) * P],
                                             tt[:, k, bass.ds(i * (GT * P) + q * GH, GH)], start=(k == 0), stop=(k == KD - 1))
                            m.then_inc(s_a.sem, 1)

                    def down(i, e):
                        for j in range(GT):
                            item = GT * (e + 1) + j
                            if j == 0:
                                s_act.wait(t, i * (UE * EXPERTS) + UE * (e + 1))
                            s_dve.wait(t, i * ITEMS + item - 3)
                            for k in range(KD):
                                m = t.matmul(ps[4 + item % 4][:, 0:D], hid[e % 2][:, k, j * P:(j + 1) * P], w2[:, e, k, :],
                                             start=(k == 0), stop=(k == KD - 1))
                            m.then_inc(s_b.sem, 1)

                    with t.Fori(0, NG) as i:
                        s_c.wait(t, i + 1)
                        s_dve.wait(t, i * ITEMS)
                        for j in range(GT):
                            m = t.transpose(ps[4 + j // 4][0:EXPERTS, (j % 4) * P:(j % 4 + 1) * P], cst[:, j, :], ident[:])
                        m.then_inc(s_pe.sem, 1)
                        up(i, 0)
                        for j in range(GT):
                            if j == 0:
                                s_d.wait(t, i * 2 + 2)
                            s_dve.wait(t, i * ITEMS + max(j - 3, 0))
                            t.matmul(ps[4 + j % 4][:, 0:D], ctt[:, j, :], b2[:], start=True, stop=True).then_inc(s_f.sem, 1)
                        for e in range(EXPERTS):
                            if e + 1 < EXPERTS:
                                up(i, e + 1)
                            down(i, e)

                @b.scalar
                def _(a):
                    with a.Fori(0, NG) as i:
                        s_pe.wait(a, i)
                        a.copy(cst[:], comb[:, bass.ds(i * GT, GT), :]).then_inc(s_c.sem, 1)
                        s_pe.wait(a, i + 1)
                        s_f.wait(a, i * GT)
                        a.copy(ctt[:, 0:4, :], ps[4][0:EXPERTS, :].rearrange("p (j c) -> p j c", j=4)).then_inc(s_d.sem, 1)
                        a.copy(ctt[:, 4:GT, :], ps[5][0:EXPERTS, 0:(GT - 4) * P].rearrange("p (j c) -> p j c", j=GT - 4)).then_inc(s_d.sem, 1)
                        for e in range(EXPERTS):
                            for u in range(UE):
                                f, q = divmod(u, 2)
                                s_a.wait(a, i * (UE * EXPERTS) + UE * e + u + 1)
                                if e >= 2:
                                    s_b.wait(a, i * (GT * EXPERTS) + GT * (e - 1))
                                a.activation(hid[e % 2][:, f, q * GH:(q + 1) * GH], ps[u][:, 0:GH], ACT.Gelu,
                                             bias=b1[:, e, f:f + 1]).then_inc(s_act.sem, 1)

                @b.vector
                def _(v):
                    with v.Fori(0, NG) as i:
                        for item in range(ITEMS):
                            e, j = divmod(item, GT)
                            e, n, bank = e - 1, i * GT + j, ps[4 + item % 4][:, 0:D]
                            if e < 0:
                                s_f.wait(v, i * GT + j + 1)
                                if j == 0:
                                    s_e.wait(v, i)
                                v.tensor_tensor(xs[:, n, :], xs[:, n, :], bank, ALU.add).then_inc(s_dve.sem, 1)
                            else:
                                s_b.wait(v, i * (GT * EXPERTS) + GT * e + j + 1)
                                s_dve.wait(v, i * ITEMS + item - GT + 1)
                                v.scalar_tensor_tensor(xs[:, n, :], bank, comb[:, n, e:e + 1], xs[:, n, :],
                                                       ALU.mult, ALU.add).then_inc(s_dve.sem, 1)
                        s_dve.wait(v, i * ITEMS + ITEMS)
                        for j in range(GT):
                            n = i * GT + j
                            m = v.bn_stats(bn6[:, n, :], xs[:, n, :])
                        m.then_inc(s_e.sem, 1)
            for s in (s_c, s_e, s_pe):
                s.after(NG)
            s_d.after(2 * NG)
            s_f.after(NT)
            s_a.after(NG * UE * EXPERTS)
            s_act.after(NG * UE * EXPERTS)
            s_b.after(NT * EXPERTS)
            s_dve.after(NG * ITEMS)
        finish_statistics()

        with ExitStack() as l1:
            weight = sb("weight", [P, STEPS, HEADS], F32, l1)
            flat = STEPS * HEADS
            sc = weight[:].rearrange("p s h -> p (s h)")

            with ExitStack() as l1a:
                sdst = sb("sdst", [P, NT, TYPES * HEADS], F32, l1a)
                scd = sb("scd", [P, STEPS, HEADS], F32, l1a)

                with ExitStack() as ph:
                    wt = sb("a_wts", [P, KD, TYPES * D], F32, ph)
                    wn = sb("a_wn", [P, TYPES, KD, D], F32, ph)
                    at = sb("a_at", [P, KD, 2 * HEADS], F32, ph)
                    wa = sb("a_wa", [P, KD, 2 * TYPES * HEADS], F32, ph)
                    xn = [sb(f"a_xn{k}", [P, D], F32, ph) for k in range(2)]
                    xnt = [sb(f"a_xnt{k}", [P, D], F32, ph) for k in range(2)]
                    rows = [sb(f"a_rows{k}", [P, TYPES, ROW], F32, ph) for k in range(2)]
                    with nc.Block() as b:
                        @b.vector
                        def _(v):
                            v.memset(at[:], 0.0).then_inc(s_dve.sem, 1)

                        @b.sync
                        def _(sp):
                            sp.dma_start(wt[:], a_wt.rearrange("(k p) r o -> p k (r o)", p=P)).then_inc(s_in.sem, 16)
                            sp.dma_start(wn[:], a_w.rearrange("r (k p) f -> p r k f", p=P)).then_inc(s_in.sem, 16)
                            s_dve.wait(sp, 1)
                            for h in range(HEADS):
                                k, r = divmod(h * HD, P)
                                for m, a in enumerate((a_src, a_dst)):
                                    sp.dma_start(at[r:r + HD, k, m * HEADS + h:m * HEADS + h + 1], a[h]).then_inc(s_in.sem, 16)
                            s_in.wait(sp, 16 * (2 + 2 * HEADS))
                    s_in.after(16 * (2 + 2 * HEADS))
                    s_dve.after(1)

                    with nc.Block() as b:
                        @b.tensor
                        def _(t):
                            for k in range(KD):
                                for r in range(TYPES):
                                    for o in range(KD):
                                        m = t.matmul(ps[k][:, r * 2 * HEADS:(r + 1) * 2 * HEADS], wn[:, r, o, k * P:(k + 1) * P],
                                                     at[:, o, :], start=(o == 0), stop=(o == KD - 1))
                                m.then_inc(s_pe.sem, 1)

                        @b.vector
                        def _(v):
                            for k in range(KD):
                                s_pe.wait(v, k + 1)
                                v.tensor_copy(wa[:, k, :].rearrange("p (m r h) -> p r m h", m=2, r=TYPES),
                                              ps[k][:, 0:2 * HEADS * TYPES].rearrange("p (r m h) -> p r m h", m=2, r=TYPES))
                    s_pe.after(KD)

                    QB = TYPES * D // 512

                    def rows_stored(engine, i, j):
                        s_ld[j % 2].wait(engine, i * (16 * (4 - j % 2)) + 16 * (j // 2))

                    with nc.Block() as b:
                        @b.vector
                        def _(v):
                            def normalise(i, j):
                                n = i * GT + j
                                s_a.wait(v, i * GT + max(j - 1, 0))
                                v.tensor_scalar(xn[j % 2][:], xs[:, n, :], mean[:, bass.ds(n, 1)], rstd[:, bass.ds(n, 1)],
                                                ALU.subtract, ALU.mult).then_inc(s_dve.sem, 1)

                            with v.Fori(0, NG) as i:
                                normalise(i, 0)
                                for j in range(GT):
                                    if j + 1 < GT:
                                        normalise(i, j + 1)
                                    for q in range(2):
                                        s_c.wait(v, i * (GT * QB) + QB * j + 2 * q + 2)
                                        if q == 0:
                                            rows_stored(v, i, j)
                                        v.tensor_copy(rows[j % 2][:, 4 * q + 2:4 * q + 4, 0:D],
                                                      ps[2 + 2 * q + 1][:].rearrange("p (r o) -> p r o", r=2)).then_inc(s_b.sem, 1)
                                    s_d.wait(v, i * GT + j + 1)
                                    v.tensor_copy(rows[j % 2][:, :, D:ROW],
                                                  ps[6 + j % 2][:, 0:64].rearrange("p (r h) -> p r h", r=TYPES)).then_inc(s_b.sem, 1)
                                    v.tensor_copy(sdst[:, i * GT + j, :], ps[6 + j % 2][:, 64:128]).then_inc(s_b.sem, 1)

                        @b.scalar
                        def _(a):
                            with a.Fori(0, NG) as i:
                                for j in range(GT):
                                    s_a.wait(a, i * GT + j + 1)
                                    s_d.wait(a, i * GT + max(j - 1, 0))
                                    a.copy(xnt[j % 2][:], ps[j % 2][:, 0:D]).then_inc(s_act.sem, 1)
                                    for q in range(2):
                                        s_c.wait(a, i * (GT * QB) + QB * j + 2 * q + 1)
                                        if q == 0:
                                            rows_stored(a, i, j)
                                        a.copy(rows[j % 2][:, 4 * q:4 * q + 2, 0:D],
                                               ps[2 + 2 * q][:].rearrange("p (r o) -> p r o", r=2)).then_inc(s_f.sem, 1)

                        @b.tensor
                        def _(t):
                            def turn_rows(i, j):
                                s_dve.wait(t, i * GT + j + 1)
                                s_act.wait(t, i * GT + max(j - 1, 0))
                                for k in range(KD):
                                    m = t.transpose(ps[j % 2][:, k * P:(k + 1) * P], xn[j % 2][:, k * P:(k + 1) * P], ident[:])
                                m.then_inc(s_a.sem, 1)

                            with t.Fori(0, NG) as i:
                                turn_rows(i, 0)
                                for j in range(GT):
                                    s_act.wait(t, i * GT + j + 1)
                                    for q in range(QB):
                                        if q % 2 == 0:
                                            s_f.wait(t, i * (2 * GT) + max(2 * j + q // 2 - 1, 0))
                                        else:
                                            s_b.wait(t, i * (4 * GT) + max(4 * j + q // 2 - 3, 0))
                                        for k in range(KD):
                                            m = t.matmul(ps[2 + q][:], xnt[j % 2][:, k * P:(k + 1) * P],
                                                         wt[:, k, q * 512:(q + 1) * 512], start=(k == 0), stop=(k == KD - 1))
                                        m.then_inc(s_c.sem, 1)
                                        if q == 1 and j + 1 < GT:
                                            turn_rows(i, j + 1)
                                    s_b.wait(t, i * (4 * GT) + max(4 * j - 4, 0))
                                    for k in range(KD):
                                        m = t.matmul(ps[6 + j % 2][:, 0:P], xnt[j % 2][:, k * P:(k + 1) * P], wa[:, k, :],
                                                     start=(k == 0), stop=(k == KD - 1))
                                    m.then_inc(s_d.sem, 1)

                        @b.sync
                        def _(sp):
                            view = t_msg.rearrange("(n p r) w -> n p r w", p=P, r=TYPES)
                            with sp.Fori(0, NG) as i:
                                for j in range(GT):
                                    s_b.wait(sp, i * (4 * GT) + 4 * j + 4)
                                    s_f.wait(sp, i * (2 * GT) + 2 * j + 2)
                                    sp.dma_start(view[i * GT + j], rows[j % 2][:]).then_inc(s_ld[j % 2].sem, 16)
                            s_ld[0].wait(sp, 16 * 4 * NG)
                            s_ld[1].wait(sp, 16 * 3 * NG)
                    for s in (s_dve, s_a, s_act, s_d):
                        s.after(NT)
                    s_b.after(4 * NT)
                    s_f.after(2 * NT)
                    s_c.after(QB * NT)
                    s_ld[0].after(16 * 4 * NG)
                    s_ld[1].after(16 * 3 * NG)

                with ExitStack() as ph:
                    HV = 4
                    RT = STEPS // (8 * HV)
                    ring = sb("a_ring", [P, 8 * HV, ROW], F32, ph)
                    hot = [sb(f"a_hot{k}", [P, 8, P], F32, ph) for k in range(2)]
                    hott = sb("a_hott", [P, 8, P], F32, ph)
                    tmask = sb("a_tmask", [P, 8, TYPES], F32, ph)
                    prod = sb("a_prod", [P, 8, TYPES, HEADS], F32, ph)
                    edst = sb("a_edst", [P, 8, HEADS], F32, ph)
                    esum = sb("a_esum", [P, 8, HEADS], F32, ph)
                    iota8 = sb("a_iota8", [P, TYPES], F32, ph)
                    valid = sb("valid", [P, STEPS], F32, ph)
                    with nc.Block() as b:
                        @b.vector
                        def _(v):
                            c = Chain(v, s_dve)
                            c.did(v.tensor_scalar(iota8[:], iota8m[:], 8.0, None, ALU.add))
                            c.step(v.tensor_scalar(valid[:], dloc[:, 0:STEPS], 0.0, None, ALU.is_ge))
                            c.step(v.scalar_tensor_tensor(valid[:], dloc[:, 0:STEPS], float(P - 1), valid[:], ALU.is_le, ALU.mult))
                    s_dve.after(3)

                    with nc.Block() as b:
                        pool, stage_half = gather_turns(t_msg, lambda j: ring[:, j, :], idx3, HV)

                        def rows_used(engine, i, h):
                            s_used.wait(engine, i * HV + h + 1)

                        @b.gpsimd
                        def _(g):
                            pool(g, rows_used)

                        @b.sync
                        def _(sp):
                            def store(i, h):
                                for j in range(8 * h, 8 * h + 8):
                                    s_row[j].wait(sp, i * 16 + 16)
                                sp.dma_start(t_path[i * HV + h].rearrange("p (s f) -> p s f", s=8),
                                             ring[:, 8 * h:8 * h + 8, 0:D]).then_inc(s_ld[h].sem, 16)

                            def hand_back(i, h):
                                s_ld[h].wait(sp, i * 16 + 16)
                                s_c.wait(sp, i * HV + h + 1)
                                sp.sem_inc(s_used.sem, 1)

                            sp.sem_inc(s_used.sem, HV)
                            with sp.Fori(0, RT) as i:
                                for h in range(HV):
                                    store(i, h)
                                    if h:
                                        hand_back(i, h - 1)
                                hand_back(i, HV - 1)

                        @b.scalar
                        def _(a):
                            for h in range(2):
                                stage_half(a, rows_used, 0, h)
                            with a.Fori(0, RT) as i:
                                for h in range(HV):
                                    stage_half(a, rows_used, i + (h + 2) // HV, (h + 2) % HV)
                                    q = i * HV + h
                                    s_a.wait(a, q + 1)
                                    s_b.wait(a, q)
                                    for k in range(2):
                                        a.copy(hott[:, 4 * k:4 * k + 4, :],
                                               ps[k][:].rearrange("p (s c) -> p s c", s=4)).then_inc(s_act.sem, 1)
                                    for j in range(8 * h, 8 * h + 8):
                                        s_row[j].wait(a, i * 16 + 16)
                                    a.copy(scd[:, bass.ds(q * 8, 8), :],
                                           ring[:, 8 * h:8 * h + 8, D:ROW]).then_inc(s_c.sem, 1)

                        @b.tensor
                        def _(t):
                            with t.Fori(0, RT) as i:
                                for h in range(HV):
                                    q = i * HV + h
                                    s_hot.wait(t, q + 1)
                                    s_act.wait(t, q * 2)
                                    for j in range(8):
                                        m = t.transpose(ps[j // 4][:, (j % 4) * P:(j % 4 + 1) * P], hot[h % 2][:, j, :], ident[:])
                                    m.then_inc(s_a.sem, 1)
                                    tiles = load_registers(t, f"s{h}", nrow, q * 8, 8, NT - 1)
                                    s_act.wait(t, q * 2 + 2)
                                    s_d.wait(t, i * HV + max(h - 1, 0))
                                    for j in range(8):
                                        m = t.matmul(ps[2 + h % 2][:, j * 64:(j + 1) * 64], hott[:, j, :], sdst[:, tiles[j], :],
                                                     start=True, stop=True)
                                    m.then_inc(s_b.sem, 1)

                        @b.vector
                        def _(v):
                            wide = [P, 8, TYPES, HEADS]
                            build_hot(v, hot[0][:], 0).then_inc(s_hot.sem, 1)
                            with v.Fori(0, RT) as i:
                                for h in range(HV):
                                    q = i * HV + h
                                    s_a.wait(v, q)
                                    build_hot(v, hot[1 - h % 2][:], q * 8 + 8).then_inc(s_hot.sem, 1)
                                    s_d.wait(v, q)
                                    v.tensor_tensor(tmask[:], typf[:, bass.ds(q * 8, 8)].unsqueeze(2).to_broadcast([P, 8, TYPES]),
                                                    iota8[:].unsqueeze(1).to_broadcast([P, 8, TYPES]), ALU.is_equal).then_inc(s_e.sem, 1)
                                    s_e.wait(v, q + 1)
                                    s_b.wait(v, q + 1)
                                    s_f.wait(v, q)
                                    v.tensor_tensor(prod[:], ps[2 + h % 2][:].rearrange("p (s r h) -> p s r h", s=8, r=TYPES),
                                                    tmask[:].unsqueeze(3).to_broadcast(wide), ALU.mult).then_inc(s_d.sem, 1)
                                    s_d.wait(v, q + 1)
                                    s_dve.wait(v, q * 3)
                                    v.tensor_reduce(edst[:], prod[:].rearrange("p s r h -> p s h r"), AX, ALU.add).then_inc(s_f.sem, 1)
                                    s_c.wait(v, q + 1)
                                    v.tensor_tensor(esum[:], scd[:, bass.ds(q * 8, 8), :],
                                                    valid[:, bass.ds(q * 8, 8)].unsqueeze(2).to_broadcast([P, 8, HEADS]),
                                                    ALU.mult).then_inc(s_dve.sem, 1)
                                    s_f.wait(v, q + 1)
                                    s_dve.wait(v, q * 3 + 1)
                                    v.tensor_tensor(esum[:], esum[:], edst[:], ALU.add).then_inc(s_dve.sem, 1)
                                    s_dve.wait(v, q * 3 + 2)
                                    v.scalar_tensor_tensor(weight[:, bass.ds(q * 8, 8), :], esum[:], 0.2, esum[:],
                                                           ALU.mult, ALU.max).then_inc(s_dve.sem, 1)
                    s_used.after(STEPS // 8 + HV)
                    after_gathers(HV)
                    s_stage.after(2)
                    s_hot.after(1)
                    for k in range(HV):
                        s_ld[k].after(16 * RT)
                    for s in (s_a, s_b, s_c, s_d, s_e, s_f, s_hot):
                        s.after(STEPS // 8)
                    s_act.after(2 * (STEPS // 8))
                    s_dve.after(3 * (STEPS // 8))

                with ExitStack() as ph:
                    score = sb("score", [P, CW], F32, ph)
                    keyt = sb("keyt", [P, CW], F32, ph)
                    stg = [sb(f"stg{k}", [P, 4, P], F32, ph) for k in range(2)]
                    stk = [sb(f"stk{k}", [P, 4, P], F32, ph) for k in range(2)]
                    carry = [sb(f"carry{k}", [1, P], F32, ph) for k in range(13)]
                    cols = sb("cols", [P, 2], F32, ph)
                    Q = CS // 4

                    def by_chunk(a, i, n=HEADS):
                        return a.rearrange("p (c j) h -> p j c h", c=CH)[:, bass.ds(i * 4, 4), :, :]

                    def quads(engine, body):
                        with engine.Fori(0, Q // 2) as i:
                            for k in range(2):
                                body(i * 2 + k, k)
                        body(Q - 1, 0)

                    with nc.Block() as b:
                        @b.vector
                        def _(v):
                            def body(i, k):
                                s_a.wait(v, i - k)
                                v.tensor_copy(stg[k][:].rearrange("p j (c h) -> p j c h", c=CH), by_chunk(weight[:], i)).then_inc(s_dve.sem, 1)
                                v.tensor_copy(stk[k][:].rearrange("p j (c h) -> p j c h", c=CH),
                                              by_chunk(key[:, 0:STEPS].unsqueeze(2).to_broadcast([P, STEPS, HEADS]), i)).then_inc(s_dve.sem, 1)
                            quads(v, body)

                        @b.tensor
                        def _(t):
                            def body(i, k):
                                s_dve.wait(t, i * 2 + 2)
                                s_act.wait(t, (i - k) * 2)
                                for m, s in enumerate((stg[k], stk[k])):
                                    for j in range(4):
                                        last = t.transpose(ps[2 * k + m][:, j * P:(j + 1) * P], s[:, j, :], ident[:])
                                last.then_inc(s_a.sem, 1)
                            quads(t, body)

                        @b.scalar
                        def _(a):
                            def body(i, k):
                                s_a.wait(a, i + 1)
                                a.copy(score[:, bass.ds(i * 512, 512)], ps[2 * k][:]).then_inc(s_act.sem, 1)
                                a.copy(keyt[:, bass.ds(i * 512, 512)], ps[2 * k + 1][:]).then_inc(s_act.sem, 1)
                            quads(a, body)
                    s_a.after(Q)
                    s_dve.after(2 * Q)
                    s_act.after(2 * Q)

                    same, seg = sc, scd[:].rearrange("p s h -> p (s h)")
                    kf, kl, lf, fb, one, link, linkr, fwd, bwd, left, right, lcol, rcol = (c[:] for c in carry)
                    hc = "a (h c) -> a h c"

                    def r3(a):
                        return a.rearrange(hc, h=HEADS)

                    vector_steps = []
                    with nc.Block() as b:
                        @b.vector
                        def _(v):
                            c = Chain(v, s_dve)
                            c.did(v.memset(same[:, 0:1], 0.0))
                            c.step(v.tensor_tensor(same[:, 1:CW], keyt[:, 1:CW], keyt[:, 0:CW - 1], ALU.is_equal))
                            c.step(v.tensor_tensor_scan(seg, same, score[:], 0.0, ALU.mult, ALU.max))
                            c.step(v.tensor_copy(cols[:, 0:1], seg[:, CW - 1:CW]))
                            c.step(v.tensor_tensor_scan(seg[:, 0:CW - 1][:, ::-1], same[:, 1:CW][:, ::-1], seg[:, 0:CW - 1][:, ::-1],
                                                        seg[:, CW - 1:CW], ALU.mult, ALU.max))
                            s_pe.wait(v, 1)
                            for k, r in enumerate((kf, kl, lf, fb)):
                                c.did(v.tensor_copy(r3(r), ps[0][0:1, k * P:(k + 1) * P].rearrange("a (c h) -> a h c", h=HEADS)))
                            for r in (link, linkr, left, right):
                                c.did(v.memset(r, 0.0))
                            c.hold()
                            c.step(v.tensor_tensor(one, kf, kl, ALU.is_equal))
                            c.did(v.tensor_tensor(r3(link)[:, :, 1:CH], r3(kf)[:, :, 1:CH], r3(kl)[:, :, 0:CH - 1], ALU.is_equal))
                            c.did(v.tensor_tensor(r3(linkr)[:, :, 0:CH - 1], r3(kf)[:, :, 1:CH], r3(kl)[:, :, 0:CH - 1], ALU.is_equal))
                            c.hold()
                            c.did(v.tensor_tensor(lcol, one, link, ALU.mult))
                            c.did(v.tensor_tensor(rcol, one, linkr, ALU.mult))
                            c.hold()
                            c.did(v.tensor_tensor_scan(fwd, lcol, lf, 0.0, ALU.mult, ALU.max))
                            c.did(v.tensor_tensor_scan(bwd[:, ::-1], rcol[:, ::-1], fb[:, ::-1], 0.0, ALU.mult, ALU.max))
                            c.hold()
                            c.did(v.tensor_tensor(r3(left)[:, :, 1:CH], r3(link)[:, :, 1:CH], r3(fwd)[:, :, 0:CH - 1], ALU.mult))
                            c.did(v.tensor_tensor(r3(right)[:, :, 0:CH - 1], r3(linkr)[:, :, 0:CH - 1], r3(bwd)[:, :, 1:CH], ALU.mult))
                            c.hold()
                            c.did(v.tensor_copy(lcol.rearrange("a (c h) -> a c h", h=HEADS), left.rearrange("a (h c) -> a c h", h=HEADS)))
                            c.did(v.tensor_copy(rcol.rearrange("a (c h) -> a c h", h=HEADS), right.rearrange("a (h c) -> a c h", h=HEADS)))
                            c.hold()
                            v.sem_inc(s_a.sem, 1)
                            s_pe.wait(v, 2)
                            c.step(v.tensor_copy(cols[:], ps[1][:, 0:2]))
                            for k, at_ in ((0, slice(0, 1)), (1, slice(CW - 1, CW))):
                                c.step(v.tensor_scalar(same, keyt[:], keyt[:, at_], cols[:, k:k + 1], ALU.is_equal, ALU.mult))
                                c.step(v.tensor_tensor(seg, seg, same, ALU.max))
                            c.step(v.tensor_tensor(score[:], score[:], seg, ALU.subtract))
                            vector_steps.append(c.n)

                        @b.tensor
                        def _(t):
                            s_dve.wait(t, 5)
                            for k, a in enumerate((keyt[:, 0:1], keyt[:, CW - 1:CW], cols[:, 0:1], seg[:, 0:1])):
                                m = t.transpose(ps[0][0:1, k * P:(k + 1) * P], a, ident[:])
                            m.then_inc(s_pe.sem, 1)
                            s_a.wait(t, 1)
                            t.transpose(ps[1][:, 0:1], lcol, ident[0:1, 0:1])
                            t.transpose(ps[1][:, 1:2], rcol, ident[0:1, 0:1]).then_inc(s_pe.sem, 1)
                    s_dve.after(vector_steps[0])
                    s_a.after(1)
                    s_pe.after(2)

                    with nc.Block() as b:
                        @b.scalar
                        def _(a):
                            def body(i, k):
                                s_a.wait(a, i - k)
                                a.activation(stg[k][:].rearrange("p j c -> p (j c)"), score[:, bass.ds(i * 512, 512)],
                                             ACT.Exp).then_inc(s_act.sem, 1)
                            quads(a, body)

                        @b.tensor
                        def _(t):
                            def body(i, k):
                                s_act.wait(t, i + 1)
                                s_dve.wait(t, i - k)
                                for j in range(4):
                                    last = t.transpose(ps[k][:, j * P:(j + 1) * P], stg[k][:, j, :], ident[:])
                                last.then_inc(s_a.sem, 1)
                            quads(t, body)

                        @b.vector
                        def _(v):
                            def body(i, k):
                                s_a.wait(v, i + 1)
                                v.tensor_copy(by_chunk(weight[:], i),
                                              ps[k][:].rearrange("p (j c h) -> p j c h", j=4, c=CH)).then_inc(s_dve.sem, 1)
                            quads(v, body)
                    s_a.after(Q)
                    s_act.after(Q)
                    s_dve.after(Q)

            with ExitStack() as ph:
                acc = sb("a_acc", [P, NT, ROW], F32, ph)
                raws = [sb(f"a_raw{k}", [P, 8, D], F32, ph) for k in range(2)]
                msgs = [sb(f"a_msg{k}", [P, 8, ROW], F32, ph) for k in range(2)]
                hot = [sb(f"a_hot2{k}", [P, 8, P], F32, ph) for k in range(2)]
                dst8 = [sb(f"a_dst8{k}", [P, 8], F32, ph) for k in range(2)]

                def turns(engine, body):
                    with engine.Fori(0, TURNS - 1) as i:
                        for h in range(2):
                            body(i, h, True)
                    for h in range(2):
                        body(TURNS - 1, h, h == 0)

                with nc.Block() as b:
                    @b.sync
                    def _(sp):
                        def body(i, h, more):
                            s_a.wait(sp, i * 2 + max(h - 1, 0))
                            sp.dma_start(raws[h][:].rearrange("p s f -> p (s f)"), t_path[i * 2 + h]).then_inc(s_ld[h].sem, 16)
                        turns(sp, body)

                    @b.scalar
                    def _(a):
                        def body(i, h, more):
                            s_used.wait(a, i * 16 + 8 * h + 8)
                            a.copy(dst8[h][:], dloc[:, bass.ds(i * 16 + 8 * h, 8)]).then_inc(s_act.sem, 1)
                            a.copy(msgs[h][:, :, D:ROW], weight[:, bass.ds(i * 16 + 8 * h, 8), :]).then_inc(s_act.sem, 1)
                        turns(a, body)

                    @b.gpsimd
                    def _(g):
                        def body(i, h, more):
                            s_act.wait(g, i * 4 + 2 * h + 1)
                            for j in range(8):
                                m = g.tensor_scalar(hot[h][:, j, :], iota[:], dst8[h][:, j:j + 1], None, ALU.is_equal)
                            m.then_inc(s_hot.sem, 1)
                        turns(g, body)

                    @b.tensor
                    def _(t):
                        t.sem_inc(s_used.sem, 16)

                        def body(i, h, more):
                            s_hot.wait(t, i * 2 + h + 1)
                            s_a.wait(t, i * 2 + h + 1)
                            s_act.wait(t, i * 4 + 2 * h + 2)
                            for j in range(8 * h, 8 * h + 8):
                                s_added.wait(t, i * 16 + j + 1)
                                t.matmul(ps[j % 8][:, 0:ROW], hot[h][:, j % 8, :], msgs[h][:, j % 8, :],
                                         start=True, stop=True).then_inc(s_used.sem, 1)
                        turns(t, body)

                    @b.vector
                    def _(v):
                        def weigh(i, h):
                            s_ld[h].wait(v, i * 16 + 16)
                            s_used.wait(v, i * 16 + 8 * h + 8)
                            v.tensor_tensor(msgs[h][:, :, 0:D].rearrange("p s (h d) -> p s h d", h=HEADS),
                                            raws[h][:].rearrange("p s (h d) -> p s h d", h=HEADS),
                                            weight[:, bass.ds(i * 16 + 8 * h, 8), :].unsqueeze(3).to_broadcast([P, 8, HEADS, HD]),
                                            ALU.mult).then_inc(s_a.sem, 1)

                        def body(i, h, more):
                            if more:
                                weigh(i + h, 1 - h)
                            tiles = load_registers(v, f"m{h}{isinstance(i, int)}", nrow, i * 16 + 8 * h, 8, NT - 1)
                            for j in range(8 * h, 8 * h + 8):
                                a_n = acc[:, tiles[j % 8], :]
                                s_used.wait(v, i * 16 + j + 17)
                                s_added.wait(v, i * 16 + j + 8)
                                v.tensor_tensor(a_n, a_n, ps[j % 8][:, 0:ROW], ALU.add).then_inc(s_added.sem, 1)

                        v.memset(acc[:], 0.0).then_inc(s_added.sem, 8)
                        weigh(0, 0)
                        turns(v, body)
                s_a.after(2 * TURNS)
                s_act.after(4 * TURNS)
                s_hot.after(2 * TURNS)
                s_used.after(STEPS + 16)
                s_added.after(STEPS + 8)
                s_ld[0].after(16 * TURNS)
                s_ld[1].after(16 * TURNS)

                with nc.Block() as b:
                    @b.vector
                    def _(v):
                        c = Chain(v, s_dve)
                        den, num = acc[:, :, D:ROW], acc[:, :, 0:D]
                        c.step(v.tensor_scalar(den, den, 1e-12, None, ALU.add))
                        c.step(v.reciprocal(den, den))
                        nh = num.rearrange("p n (h d) -> p n h d", h=HEADS)
                        c.step(v.tensor_tensor(nh, nh, den.unsqueeze(3).to_broadcast([P, NT, HEADS, HD]), ALU.mult))
                        c.step(v.tensor_tensor(xs[:], xs[:], num, ALU.add))
                s_dve.after(4)
        with nc.Block() as b:
            @b.vector
            def _(v):
                row_statistics(v)
        finish_statistics()

        with ExitStack() as ph:
            FC = FF // P
            tt = sb("v_t", [P, KD, NPAD], F32, ph)
            w1 = [sb(f"f_w1s{k}", [P, KD, FF], F32, ph) for k in range(2)]
            w2 = [sb(f"f_w2s{k}", [P, FC, D], F32, ph) for k in range(2)]
            b1 = [sb(f"f_b1s{k}", [P, FC], F32, ph) for k in range(2)]
            b2 = [sb(f"f_b2s{k}", [P, D], F32, ph) for k in range(2)]
            gamma = sb("gamma", [P, D], F32, ph)
            beta = sb("beta", [P, D], F32, ph)
            wr = sb("f_wrs", [P, KD, EXPERTS], F32, ph)
            br = sb("f_brs", [1, EXPERTS], F32, ph)
            vmean = sb("vmean", [P, KD], F32, ph)
            prob = sb("f_prob", [1, 1, EXPERTS], F32, ph)
            load = sb("f_load", [1, 1, EXPERTS], F32, ph)
            one1, one2, tmp8 = (sb(f"f_{k}", [1, 1, EXPERTS], F32, ph) for k in ("one1", "one2", "tmp8"))
            top = sb("f_top", [1, 2], F32, ph)
            sel = sb("f_sel", [1, 2], F32, ph)
            sel_i = sb("f_seli", [1, 4], I32, ph)
            total = sb("f_total", [1, 1], F32, ph)
            wsel = sb("f_wsel", [P, 2], F32, ph)
            xn = [sb(f"f_xn{k}", [P, D], F32, ph) for k in range(2)]
            with nc.Block() as b:
                @b.sync
                def _(sp):
                    sp.dma_start(wr[:], f_wr.rearrange("(k p) e -> p k e", p=P)).then_inc(s_in.sem, 16)
                    sp.dma_start(br[:], f_br).then_inc(s_in.sem, 16)
                    sp.dma_start(gamma[:], f_gamma.to_broadcast([P, D])).then_inc(s_in.sem, 16)
                    sp.dma_start(beta[:], f_beta.to_broadcast([P, D])).then_inc(s_in.sem, 16)
                    s_in.wait(sp, 64)

                @b.vector
                def _(v):
                    with v.Fori(0, NG) as i:
                        for j in range(GT):
                            n = i * GT + j
                            s_a.wait(v, i * GT + max(j - 1, 0))
                            v.tensor_scalar(xn[j % 2][:], xs[:, n, :], mean[:, bass.ds(n, 1)], rstd[:, bass.ds(n, 1)],
                                            ALU.subtract, ALU.mult).then_inc(s_dve.sem, 1)

                @b.tensor
                def _(t):
                    with t.Fori(0, NG) as i:
                        for j in range(GT):
                            s_dve.wait(t, i * GT + j + 1)
                            s_act.wait(t, i * GT + max(j - 3, 0))
                            for k in range(KD):
                                m = t.transpose(ps[j % 4][:, k * P:(k + 1) * P], xn[j % 2][:, k * P:(k + 1) * P], ident[:])
                            m.then_inc(s_a.sem, 1)

                @b.scalar
                def _(a):
                    with a.Fori(0, NG) as i:
                        for j in range(GT):
                            s_a.wait(a, i * GT + j + 1)
                            a.copy(tt[:, :, bass.ds((i * GT + j) * P, P)],
                                   ps[j % 4][:, 0:D].rearrange("p (k c) -> p k c", k=KD)).then_inc(s_act.sem, 1)
            s_in.after(64)
            for s in (s_dve, s_a, s_act):
                s.after(NT)

            vector_steps = []
            with nc.Block() as b:
                @b.vector
                def _(v):
                    c = Chain(v, s_dve)
                    c.step(v.tensor_reduce(vmean[:], tt[:, :, 0:NODES], AX, ALU.add))
                    c.did(v.tensor_scalar(vmean[:], vmean[:], 1.0 / NODES, None, ALU.mult))
                    s_pe.wait(v, 1)
                    pr, ld = prob[:], load[:]
                    c.step(v.tensor_tensor(pr[:, 0, :], ps[0][0:1, 0:EXPERTS], br[:], ALU.add))

                    def softmax(x, nth):
                        c.step(v.tensor_reduce(total[:], x, AX, ALU.max))
                        c.step(v.tensor_scalar(x, x, total[:, 0:1], None, ALU.subtract))
                        v.sem_inc(s_b.sem, 1)
                        s_act.wait(v, nth)
                        c.step(v.tensor_reduce(total[:], x, AX, ALU.add))
                        c.step(v.reciprocal(total[:], total[:]))
                        c.step(v.tensor_scalar(x, x, total[:, 0:1], None, ALU.mult))

                    softmax(pr[:, 0, :], 1)
                    c.step(v.tensor_scalar(ld, pr, float(NODES), None, ALU.mult))
                    c.step(v.reciprocal(ld, ld))
                    c.step(v.tensor_scalar(ld, ld, CAPACITY, 1.0, ALU.mult, ALU.min))
                    c.step(v.tensor_tensor(pr, pr, ld, ALU.mult))
                    softmax(pr[:, 0, :], 2)
                    first_two(c, pr, iota8m[0:1, :].unsqueeze(1), one1[:], one2[:], top[:, 0:1], top[:, 1:2],
                              sel[:, 0:1], sel[:, 1:2], tmp8[:], 1)
                    c.step(v.tensor_scalar(sel[:], sel[:], float(EXPERTS), None, ALU.add))
                    c.step(v.tensor_copy(sel_i[:, 0:2], sel[:]))
                    v.sem_inc(s_c.sem, 1)
                    softmax(top[:], 3)
                    v.sem_inc(s_d.sem, 1)
                    s_pe.wait(v, 2)
                    c.step(v.tensor_copy(wsel[:], ps[1][:, 0:2]))
                    s_in.wait(v, 16 * 8)
                    c.step(v.tensor_scalar(b2[0][:], b2[0][:], wsel[:, 0:1], None, ALU.mult))
                    c.step(v.scalar_tensor_tensor(b2[0][:], b2[1][:], wsel[:, 1:2], b2[0][:], ALU.mult, ALU.add))
                    vector_steps.append(c.n)

                @b.scalar
                def _(a):
                    for k, x in enumerate((prob[:, 0, :], prob[:, 0, :], top[:])):
                        s_b.wait(a, k + 1)
                        a.activation(x, x, ACT.Exp).then_inc(s_act.sem, 1)

                @b.tensor
                def _(t):
                    s_dve.wait(t, 2)
                    for k in range(KD):
                        m = t.matmul(ps[0][0:1, 0:EXPERTS], vmean[:, k:k + 1], wr[:, k, :], start=(k == 0), stop=(k == KD - 1))
                    m.then_inc(s_pe.sem, 1)
                    s_d.wait(t, 1)
                    t.matmul(ps[1][:, 0:2], ones[0:1, :], top[:], start=True, stop=True).then_inc(s_pe.sem, 1)

                @b.sync
                def _(sp):
                    s_c.wait(sp, 1)
                    chosen = load_registers(sp, "expert", sel_i, 0, 2, EXPERTS - 1)
                    for k, e in enumerate(chosen):
                        sp.dma_start(w1[k][:], f_w1[e].rearrange("(k p) f -> p k f", p=P)).then_inc(s_in.sem, 16)
                        sp.dma_start(w2[k][:], f_w2[e].rearrange("(k p) f -> p k f", p=P)).then_inc(s_in.sem, 16)
                        sp.dma_start(b1[k][:], f_b1[e]).then_inc(s_in.sem, 16)
                        sp.dma_start(b2[k][:], f_b2[e].to_broadcast([P, D])).then_inc(s_in.sem, 16)
                    s_in.wait(sp, 16 * 8)
            s_in.after(16 * 8)
            s_dve.after(vector_steps[0])
            s_act.after(3)
            s_b.after(3)
            s_c.after(1)
            s_d.after(1)
            s_pe.after(2)

            UE = 2 * FC
            hid = [sb(f"f_hid{k}", [P, FC, GT * P], F32, ph) for k in range(1)]
            ov = sb("f_ov", [P, GT, D], F32, ph)
            vbn = sb("f_vbn", [P, GT, 6], F32, ph)
            vm, vr, vt = (sb(f"f_v{k}", [P, GT], F32, ph) for k in "mrt")
            res = sb("f_res", [P, GT, D], F32, ph)
            with nc.Block() as b:
                @b.tensor
                def _(t):
                    with t.Fori(0, NG) as i:
                        for e in range(2):
                            for u in range(UE):
                                f, q = divmod(u, 2)
                                s_act.wait(t, i * (2 * UE) + max(UE * e + u - 3, 0))
                                for k in range(KD):
                                    m = t.matmul(ps[u % 4][:, 0:GH], w1[e][:, k, f * P:(f + 1) * P],
                                                 tt[:, k, bass.ds(i * (GT * P) + q * GH, GH)], start=(k == 0), stop=(k == KD - 1))
                                m.then_inc(s_a.sem, 1)
                            s_act.wait(t, i * (2 * UE) + UE * (e + 1))
                            for j in range(GT):
                                item = GT * e + j
                                s_b.wait(t, i * (2 * GT) + max(item - 3, 0))
                                for k in range(FC):
                                    m = t.matmul(ps[4 + item % 4][:, 0:D], hid[0][:, k, j * P:(j + 1) * P], w2[e][:, k, :],
                                                 start=(k == 0), stop=(k == FC - 1))
                                m.then_inc(s_c.sem, 1)

                @b.scalar
                def _(a):
                    with a.Fori(0, NG) as i:
                        for e in range(2):
                            for u in range(UE):
                                f, q = divmod(u, 2)
                                s_a.wait(a, i * (2 * UE) + UE * e + u + 1)
                                if u == 0:
                                    s_c.wait(a, i * (2 * GT) + GT * e)
                                a.activation(hid[0][:, f, q * GH:(q + 1) * GH], ps[u % 4][:, 0:GH], ACT.Gelu,
                                             bias=b1[e][:, f:f + 1]).then_inc(s_act.sem, 1)
                        s_d.wait(a, i + 1)
                        a.activation(vr[:], vr[:], ACT.Sqrt).then_inc(s_e.sem, 1)

                chain_steps = 3 * GT + 12

                @b.vector
                def _(v):
                    with v.Fori(0, NG) as i:
                        c = Chain(v, s_dve, i * chain_steps)
                        for j in range(GT):
                            n = i * GT + j
                            c.did(v.tensor_scalar(ov[:, j, :], xs[:, n, :], mean[:, bass.ds(n, 1)], rstd[:, bass.ds(n, 1)],
                                                  ALU.subtract, ALU.mult))
                        c.hold()
                        c.step(v.tensor_tensor(ov[:], ov[:], b2[0][:].unsqueeze(1).to_broadcast([P, GT, D]), ALU.add))
                        for item in range(2 * GT):
                            e, j = divmod(item, GT)
                            s_c.wait(v, i * (2 * GT) + item + 1)
                            if e:
                                s_b.wait(v, i * (2 * GT) + item - GT + 1)
                            v.scalar_tensor_tensor(ov[:, j, :], ps[4 + item % 4][:, 0:D], wsel[:, e:e + 1], ov[:, j, :],
                                                   ALU.mult, ALU.add).then_inc(s_b.sem, 1)
                        s_b.wait(v, i * (2 * GT) + 2 * GT)
                        for j in range(GT):
                            c.did(v.bn_stats(vbn[:, j, :], ov[:, j, :]))
                        c.hold()
                        me, mo, ve, vo = (vbn[:, :, k] for k in (1, 4, 2, 5))
                        c.did(v.tensor_tensor(vm[:], me, mo, ALU.add))
                        c.did(v.tensor_tensor(vt[:], me, mo, ALU.subtract))
                        c.did(v.tensor_tensor(vr[:], ve, vo, ALU.add))
                        c.hold()
                        c.did(v.tensor_scalar(vm[:], vm[:], 0.5, None, ALU.mult))
                        c.step(v.tensor_tensor(vt[:], vt[:], vt[:], ALU.mult))
                        c.step(v.scalar_tensor_tensor(vr[:], vt[:], D / 4.0, vr[:], ALU.mult, ALU.add))
                        c.step(v.tensor_scalar(vr[:], vr[:], 1.0 / D, EPS, ALU.mult, ALU.add))
                        v.sem_inc(s_d.sem, 1)
                        s_e.wait(v, i + 1)
                        c.step(v.reciprocal(vr[:], vr[:]))
                        s_out.wait(v, i * 16)
                        for j in range(GT):
                            c.did(v.tensor_scalar(ov[:, j, :], ov[:, j, :], vm[:, j:j + 1], vr[:, j:j + 1], ALU.subtract, ALU.mult))
                        c.hold()
                        wide = [P, GT, D]
                        c.step(v.tensor_tensor(ov[:], ov[:], gamma[:].unsqueeze(1).to_broadcast(wide), ALU.mult))
                        c.step(v.tensor_tensor(ov[:], ov[:], beta[:].unsqueeze(1).to_broadcast(wide), ALU.add))
                        c.step(v.tensor_tensor(res[:], ov[:], xs[:, bass.ds(i * GT, GT), :], ALU.add))
                        assert c.n == chain_steps
                        v.sem_inc(s_f.sem, 1)

                @b.sync
                def _(sp):
                    view = out.rearrange("(g n p) f -> g p n f", p=P, n=GT)
                    with sp.Fori(0, NG) as i:
                        s_f.wait(sp, i + 1)
                        sp.dma_start(view[i], res[:]).then_inc(s_out.sem, 16)
                    s_out.wait(sp, 16 * NG)
            s_out.after(16 * NG)


def kernel(x, src, dst, edge_type_8, L0_gnn_W1, L0_gnn_b1, L0_gnn_W2, L0_gnn_b2, L0_ffn_router_w,
           L0_ffn_w1, L0_ffn_b1, L0_ffn_w2, L0_ffn_b2, L1_gnn_W, L1_gnn_attn_src, L1_gnn_attn_dst,
           L1_ffn_Wr, L1_ffn_br, L1_ffn_W1, L1_ffn_b1, L1_ffn_W2, L1_ffn_b2, L1_ffn_gamma, L1_ffn_beta):
    import numpy as np
    import concourse.bacc as bacc
    from concourse.bass_utils import run_bass_kernel_spmd

    def tiles(a, fill):
        a = np.asarray(a)
        full = np.full((ETP * P,), fill, a.dtype)
        full[:EDGES] = a
        return full.reshape(ETP, P)

    x = np.asarray(x)
    x_full = np.zeros((NPAD, D), x.dtype)
    x_full[:NODES] = x
    dst_t = tiles(dst, PAD_DST)
    arrays = {
        "x": x_full,
        "src": tiles(src, 0),
        "dst": dst_t,
        "typ": tiles(edge_type_8, 0),
        "dst_e": dst_t.T,
        "dst_first": dst_t[:, 0][None],
        "g_w1": L0_gnn_W1, "g_b1": np.asarray(L0_gnn_b1)[None], "g_w2": L0_gnn_W2, "g_b2": np.asarray(L0_gnn_b2)[None],
        "m_rw": np.asarray(L0_ffn_router_w).T,
        "m_w1": L0_ffn_w1,
        "m_b1": np.asarray(L0_ffn_b1).reshape(EXPERTS, KD, P).transpose(2, 0, 1),
        "m_w2": L0_ffn_w2, "m_b2": L0_ffn_b2,
        "a_w": L1_gnn_W,
        "a_wt": np.asarray(L1_gnn_W).transpose(2, 0, 1),
        "a_src": np.asarray(L1_gnn_attn_src)[:, :, None], "a_dst": np.asarray(L1_gnn_attn_dst)[:, :, None],
        "f_wr": L1_ffn_Wr, "f_br": np.asarray(L1_ffn_br)[None],
        "f_w1": L1_ffn_W1,
        "f_b1": np.asarray(L1_ffn_b1).reshape(EXPERTS, FF // P, P).transpose(0, 2, 1),
        "f_w2": L1_ffn_W2, "f_b2": np.asarray(L1_ffn_b2)[:, None, :],
        "f_gamma": np.asarray(L1_ffn_gamma)[None], "f_beta": np.asarray(L1_ffn_beta)[None],
    }
    nc = bacc.Bacc("TRN2", target_bir_lowering=False, num_devices=1)
    feeds, args = {}, []
    for name, a in arrays.items():
        a = np.ascontiguousarray(a)
        feeds[f"in_{name}"] = a
        args.append(nc.dram_tensor(f"in_{name}", a.shape, mybir.dt.from_np(a.dtype), kind="ExternalInput").ap())
    out = nc.dram_tensor("out", (NPAD, D), F32, kind="ExternalOutput").ap()
    gnn_ffn_kernel(nc, *args, out)
    r = run_bass_kernel_spmd(nc, [feeds], core_ids=[0])
    return r.results[0]["out"][:NODES]
```
